# Optimizing a Trainium2 kernel written in Bass

```python
import numpy as np
import jax
import jax.numpy as jnp

def _softmax(x, axis=-1):
    return jax.nn.softmax(x, axis=axis)

def _gelu(x):
    return jax.nn.gelu(x, approximate=True)

def _silu(x):
    return jax.nn.silu(x)

def _sigmoid(x):
    return jax.nn.sigmoid(x)

def _layernorm(x, axis=-1, eps=1e-05):
    m = jnp.mean(x, axis=axis, keepdims=True)
    v = jnp.var(x, axis=axis, keepdims=True)
    return (x - m) / jnp.sqrt(v + eps)

def _scatter_add(tgt, idx, src, axis=0):
    return tgt.at[idx].add(src)

def _segment_sum(src, seg, n):
    return jax.ops.segment_sum(src, seg, n)
kernel_name = 'mk_vit_tower_d2_tok_img512_r4_03a5ab'

def setup_inputs(seed: int=0):
    np.random.seed(seed)
    _w = jnp.asarray

    def _rec_inputs():
        import jax
        import jax.numpy as jnp
        _rk = jax.random.key(seed)
        x = -0.000356955 + 1 * jax.random.normal(jax.random.fold_in(_rk, 1), (64, 3, 224, 224), jnp.float32)
        return x
    x = _rec_inputs()

    def _L0_tok_setup():
        import jax, jax.numpy as jnp
        import numpy as np
        P = 16
        SHIFT = P // 2
        EPS = 1e-05

        def _shift2d(img, dy, dx):
            H, W = (img.shape[2], img.shape[3])
            pad = ((0, 0), (0, 0), (max(dy, 0), max(-dy, 0)), (max(dx, 0), max(-dx, 0)))
            z = jnp.pad(img, pad)
            return z[:, :, max(-dy, 0):max(-dy, 0) + H, max(-dx, 0):max(-dx, 0) + W]

        def _patchify(img):
            B, C, H, W = img.shape
            nH, nW = (H // P, W // P)
            t = img.reshape(B, C, nH, P, nW, P).transpose(0, 2, 4, 1, 3, 5)
            return t.reshape(B, nH * nW, C * P * P)
        key = jax.random.key(seed)
        ks = jax.random.split(key, 8)
        B, C, H, Wd = (128, 3, 224, 224)
        embed_dim = 128
        d_main = embed_dim // 2
        d_shift = embed_dim // 8
        fan_in = C * P * P
        std = 0.02
        x = jax.random.normal(ks[0], (B, C, H, Wd), dtype=jnp.float32)
        W_main = jax.random.normal(ks[1], (d_main, fan_in), dtype=jnp.float32) * std
        b_main = jnp.zeros((d_main,), dtype=jnp.float32)
        W_sx = jax.random.normal(ks[2], (d_shift, fan_in), dtype=jnp.float32) * std
        b_sx = jnp.zeros((d_shift,), dtype=jnp.float32)
        W_sy = jax.random.normal(ks[3], (d_shift, fan_in), dtype=jnp.float32) * std
        b_sy = jnp.zeros((d_shift,), dtype=jnp.float32)
        ln_g = jnp.ones((embed_dim,), dtype=jnp.float32)
        ln_b = jnp.zeros((embed_dim,), dtype=jnp.float32)
        return {'x': x, 'W_main': W_main, 'b_main': b_main, 'W_sx': W_sx, 'b_sx': b_sx, 'W_sy': W_sy, 'b_sy': b_sy, 'ln_g': ln_g, 'ln_b': ln_b}
    _L0_tok_all = _L0_tok_setup()
    _L0_tok_in = {k: v for k, v in _L0_tok_all.items() if k in ('W_main', 'b_main', 'W_sx', 'b_sx', 'W_sy', 'b_sy', 'ln_g', 'ln_b')}
    del _L0_tok_all

    def _L0_attn_setup():
        import math
        import jax, jax.numpy as jnp
        import numpy as np
        INPUT_DIM = 128
        HIDDEN_DIM = 128
        BATCH = 8
        SEQ_LEN = 1024

        def _xavier(key, shape):
            fan_out, fan_in = shape
            limit = math.sqrt(6.0 / (fan_in + fan_out))
            return jax.random.uniform(key, shape, jnp.float32, -limit, limit)
        key = jax.random.key(seed)
        kx, kA, kB, kC, kD, kWg = jax.random.split(key, 6)
        return {'x': jax.random.normal(kx, (BATCH, SEQ_LEN, INPUT_DIM), jnp.float32), 'A': jax.random.uniform(kA, (HIDDEN_DIM,), jnp.float32, 0.8, 0.95), 'B': _xavier(kB, (HIDDEN_DIM, INPUT_DIM)), 'C': _xavier(kC, (HIDDEN_DIM, HIDDEN_DIM)), 'D': _xavier(kD, (HIDDEN_DIM, INPUT_DIM)), 'Wg': _xavier(kWg, (HIDDEN_DIM, INPUT_DIM)), 'bias_h': jnp.zeros((HIDDEN_DIM,), jnp.float32), 'bias_y': jnp.zeros((HIDDEN_DIM,), jnp.float32)}
    _L0_attn_all = _L0_attn_setup()
    _L0_attn_in = {k: v for k, v in _L0_attn_all.items() if k in ('A', 'B', 'C', 'D', 'Wg', 'bias_h', 'bias_y')}
    del _L0_attn_all

    def _L0_ffn_setup():
        import jax, jax.numpy as jnp
        import numpy as np
        MARK_AX = 0
        OP_MUL = 1
        OPCODE_BASE = 2
        ALU_LO, ALU_HI = (64, 80)
        AX_CARRY_LO, AX_CARRY_HI = (96, 112)
        OUTPUT_LO, OUTPUT_HI = (128, 144)
        NIB_A, NIB_B, RESULT, OP_START = (0, 1, 2, 3)
        GE_DIM = 160
        N_POS = 8
        N_LAYERS = 7
        OPCODE = 27

        def _decode_nibble(x16):
            return jnp.argmax(x16 > 0.5, axis=-1).astype(x16.dtype)
        key = jax.random.key(seed)
        k1, k2, k3 = jax.random.split(key, 3)
        x_bd = jax.random.uniform(k1, (4, 2048, 128), dtype=jnp.float32)
        W = jax.random.normal(k2, (N_LAYERS, GE_DIM, GE_DIM), dtype=jnp.float32) * 0.05
        b = jax.random.normal(k3, (N_LAYERS, GE_DIM), dtype=jnp.float32) * 0.01
        return {'x_bd': x_bd, 'W': W, 'b': b}
    _L0_ffn_all = _L0_ffn_setup()
    _L0_ffn_in = {k: v for k, v in _L0_ffn_all.items() if k in ('W', 'b')}
    del _L0_ffn_all

    def _L1_attn_setup():
        import jax, jax.numpy as jnp
        import numpy as np
        B, T, I, H, O = (32, 128, 128, 256, 128)
        key = jax.random.key(seed)
        ks = jax.random.split(key, 7)
        s_ih = 1.0 / np.sqrt(H)
        s_lin = 1.0 / np.sqrt(H)
        return {'x': jax.random.normal(ks[0], (B, T, I), dtype=jnp.float32), 'W_ih': jax.random.uniform(ks[1], (H, I), jnp.float32, -s_ih, s_ih), 'W_hh': jax.random.uniform(ks[2], (H, H), jnp.float32, -s_ih, s_ih), 'b_ih': jax.random.uniform(ks[3], (H,), jnp.float32, -s_ih, s_ih), 'b_hh': jax.random.uniform(ks[4], (H,), jnp.float32, -s_ih, s_ih), 'W_out': jax.random.uniform(ks[5], (O, H), jnp.float32, -s_lin, s_lin), 'b_out': jax.random.uniform(ks[6], (O,), jnp.float32, -s_lin, s_lin)}
    _L1_attn_all = _L1_attn_setup()
    _L1_attn_in = {k: v for k, v in _L1_attn_all.items() if k in ('W_ih', 'W_hh', 'b_ih', 'b_hh', 'W_out', 'b_out')}
    del _L1_attn_all

    def _L1_ffn_setup():
        import jax, jax.numpy as jnp
        import numpy as np
        B, N, D, E = (8, 2048, 128, 8)
        H = 2 * D
        key = jax.random.key(seed)
        ks = jax.random.split(key, 7)
        s = 0.02
        return {'x': jax.random.normal(ks[0], (B, N, D), dtype=jnp.float32), 'W1': jax.random.normal(ks[1], (E, D, H), dtype=jnp.float32) * s, 'b1': jnp.zeros((E, H), dtype=jnp.float32), 'W2': jax.random.normal(ks[2], (E, H, D), dtype=jnp.float32) * s, 'b2': jnp.zeros((E, D), dtype=jnp.float32), 'Wg': jax.random.normal(ks[3], (D, E), dtype=jnp.float32) * s, 'bg': jnp.zeros((E,), dtype=jnp.float32)}
    _L1_ffn_all = _L1_ffn_setup()
    _L1_ffn_in = {k: v for k, v in _L1_ffn_all.items() if k in ('W1', 'b1', 'W2', 'b2', 'Wg', 'bg')}
    del _L1_ffn_all
    return {'x': x, 'L0_tok_W_main': _L0_tok_in['W_main'], 'L0_tok_b_main': _L0_tok_in['b_main'], 'L0_tok_W_sx': _L0_tok_in['W_sx'], 'L0_tok_b_sx': _L0_tok_in['b_sx'], 'L0_tok_W_sy': _L0_tok_in['W_sy'], 'L0_tok_b_sy': _L0_tok_in['b_sy'], 'L0_tok_ln_g': _L0_tok_in['ln_g'], 'L0_tok_ln_b': _L0_tok_in['ln_b'], 'L0_attn_A': _L0_attn_in['A'], 'L0_attn_B': _L0_attn_in['B'], 'L0_attn_C': _L0_attn_in['C'], 'L0_attn_D': _L0_attn_in['D'], 'L0_attn_Wg': _L0_attn_in['Wg'], 'L0_attn_bias_h': _L0_attn_in['bias_h'], 'L0_attn_bias_y': _L0_attn_in['bias_y'], 'L0_ffn_W': _L0_ffn_in['W'], 'L0_ffn_b': _L0_ffn_in['b'], 'L1_attn_W_ih': _L1_attn_in['W_ih'], 'L1_attn_W_hh': _L1_attn_in['W_hh'], 'L1_attn_b_ih': _L1_attn_in['b_ih'], 'L1_attn_b_hh': _L1_attn_in['b_hh'], 'L1_attn_W_out': _L1_attn_in['W_out'], 'L1_attn_b_out': _L1_attn_in['b_out'], 'L1_ffn_W1': _L1_ffn_in['W1'], 'L1_ffn_b1': _L1_ffn_in['b1'], 'L1_ffn_W2': _L1_ffn_in['W2'], 'L1_ffn_b2': _L1_ffn_in['b2'], 'L1_ffn_Wg': _L1_ffn_in['Wg'], 'L1_ffn_bg': _L1_ffn_in['bg']}

def reference(x, L0_tok_W_main, L0_tok_b_main, L0_tok_W_sx, L0_tok_b_sx, L0_tok_W_sy, L0_tok_b_sy, L0_tok_ln_g, L0_tok_ln_b, L0_attn_A, L0_attn_B, L0_attn_C, L0_attn_D, L0_attn_Wg, L0_attn_bias_h, L0_attn_bias_y, L0_ffn_W, L0_ffn_b, L1_attn_W_ih, L1_attn_W_hh, L1_attn_b_ih, L1_attn_b_hh, L1_attn_W_out, L1_attn_b_out, L1_ffn_W1, L1_ffn_b1, L1_ffn_W2, L1_ffn_b2, L1_ffn_Wg, L1_ffn_bg):
    import jax
    import jax.numpy as jnp

    def _L0_tok_ref(x, W_main, b_main, W_sx, b_sx, W_sy, b_sy, ln_g, ln_b):
        import jax, jax.numpy as jnp
        import numpy as np
        P = 16
        SHIFT = P // 2
        EPS = 1e-05

        def _shift2d(img, dy, dx):
            H, W = (img.shape[2], img.shape[3])
            pad = ((0, 0), (0, 0), (max(dy, 0), max(-dy, 0)), (max(dx, 0), max(-dx, 0)))
            z = jnp.pad(img, pad)
            return z[:, :, max(-dy, 0):max(-dy, 0) + H, max(-dx, 0):max(-dx, 0) + W]

        def _patchify(img):
            B, C, H, W = img.shape
            nH, nW = (H // P, W // P)
            t = img.reshape(B, C, nH, P, nW, P).transpose(0, 2, 4, 1, 3, 5)
            return t.reshape(B, nH * nW, C * P * P)

        def proj(img, W, b):
            return jnp.einsum('bnf,of->bno', _patchify(img), W) + b
        main = proj(x, W_main, b_main)
        xl = proj(_shift2d(x, 0, -SHIFT), W_sx, b_sx)
        xr = proj(_shift2d(x, 0, SHIFT), W_sx, b_sx)
        yu = proj(_shift2d(x, -SHIFT, 0), W_sy, b_sy)
        yd = proj(_shift2d(x, SHIFT, 0), W_sy, b_sy)
        tok = jnp.concatenate([main, xl, xr, yu, yd], axis=-1)
        mu = jnp.mean(tok, axis=-1, keepdims=True)
        var = jnp.mean(jnp.square(tok - mu), axis=-1, keepdims=True)
        return (tok - mu) * jax.lax.rsqrt(var + EPS) * ln_g + ln_b

    def _L0_attn_ref(x, A, B, C, D, Wg, bias_h, bias_y):
        import math
        import jax, jax.numpy as jnp
        import numpy as np
        INPUT_DIM = 128
        HIDDEN_DIM = 128
        BATCH = 8
        SEQ_LEN = 1024

        def _xavier(key, shape):
            fan_out, fan_in = shape
            limit = math.sqrt(6.0 / (fan_in + fan_out))
            return jax.random.uniform(key, shape, jnp.float32, -limit, limit)
        hidden_dim = A.shape[0]
        g = jnp.clip(jax.nn.sigmoid(jnp.einsum('bti,hi->bth', x, Wg)), 0.05, 0.95)
        xB = jnp.einsum('bti,hi->bth', x, B)
        a_coef = 1.0 - g * (1.0 - A)
        b_coef = g * (xB + bias_h)

        def step(h, ab):
            a_t, b_t = ab
            h = a_t * h + b_t
            return (h, h)
        h0 = jnp.zeros((x.shape[0], hidden_dim), x.dtype)
        _, hs = jax.lax.scan(step, h0, (jnp.swapaxes(a_coef, 0, 1), jnp.swapaxes(b_coef, 0, 1)))
        hs = jnp.swapaxes(hs, 0, 1)
        scale = 1.0 / math.sqrt(hidden_dim)
        y = (jnp.einsum('bth,oh->bto', hs, C) + jnp.einsum('bti,hi->bth', x, D) + bias_y) * scale
        return y

    def _L0_ffn_ref(x_bd, W, b):
        import jax, jax.numpy as jnp
        import numpy as np
        MARK_AX = 0
        OP_MUL = 1
        OPCODE_BASE = 2
        ALU_LO, ALU_HI = (64, 80)
        AX_CARRY_LO, AX_CARRY_HI = (96, 112)
        OUTPUT_LO, OUTPUT_HI = (128, 144)
        NIB_A, NIB_B, RESULT, OP_START = (0, 1, 2, 3)
        GE_DIM = 160
        N_POS = 8
        N_LAYERS = 7
        OPCODE = 27

        def _decode_nibble(x16):
            return jnp.argmax(x16 > 0.5, axis=-1).astype(x16.dtype)
        B, S, D = x_bd.shape
        mask = (x_bd[..., MARK_AX] >= 0.5) & (x_bd[..., OP_MUL] >= 0.5)
        a_lo = _decode_nibble(x_bd[..., ALU_LO:ALU_LO + 16])
        a_hi = _decode_nibble(x_bd[..., ALU_HI:ALU_HI + 16])
        b_lo = _decode_nibble(x_bd[..., AX_CARRY_LO:AX_CARRY_LO + 16])
        b_hi = _decode_nibble(x_bd[..., AX_CARRY_HI:AX_CARRY_HI + 16])
        op_val = x_bd[..., OPCODE_BASE + OPCODE]
        x_ge = jnp.zeros((B, S, N_POS, GE_DIM), dtype=x_bd.dtype)
        x_ge = x_ge.at[..., 0, NIB_A].set(a_lo)
        x_ge = x_ge.at[..., 1, NIB_A].set(a_hi)
        x_ge = x_ge.at[..., 0, NIB_B].set(b_lo)
        x_ge = x_ge.at[..., 1, NIB_B].set(b_hi)
        x_ge = x_ge.at[..., :, OP_START + OPCODE].set(op_val[..., None])
        h = x_ge
        for i in range(N_LAYERS):
            h = jnp.einsum('bspd,ed->bspe', h, W[i]) + b[i]
            if i < N_LAYERS - 1:
                h = jax.nn.relu(h)
        res_lo = jnp.clip(jnp.round(h[..., 0, RESULT]), 0, 15).astype(jnp.int32)
        res_hi = jnp.clip(jnp.round(h[..., 1, RESULT]), 0, 15).astype(jnp.int32)
        m = mask[..., None].astype(x_bd.dtype)
        add_lo = 2.0 * jax.nn.one_hot(res_lo, 16, dtype=x_bd.dtype) * m
        add_hi = 2.0 * jax.nn.one_hot(res_hi, 16, dtype=x_bd.dtype) * m
        out = x_bd.at[..., OUTPUT_LO:OUTPUT_LO + 16].add(add_lo)
        out = out.at[..., OUTPUT_HI:OUTPUT_HI + 16].add(add_hi)
        return out

    def _L1_attn_ref(x, W_ih, W_hh, b_ih, b_hh, W_out, b_out):
        import jax, jax.numpy as jnp
        import numpy as np
        B, T, I, H, O = (32, 128, 128, 256, 128)
        xp = jnp.einsum('bti,hi->bth', x, W_ih) + b_ih + b_hh
        h0 = jnp.zeros((x.shape[0], W_hh.shape[0]), dtype=x.dtype)

        def step(h, xp_t):
            h = jax.nn.relu(xp_t + h @ W_hh.T)
            return (h, h)
        _, hs = jax.lax.scan(step, h0, jnp.swapaxes(xp, 0, 1))
        hs = jnp.swapaxes(hs, 0, 1)
        return jnp.einsum('bth,oh->bto', hs, W_out) + b_out

    def _L1_ffn_ref(x, W1, b1, W2, b2, Wg, bg):
        import jax, jax.numpy as jnp
        import numpy as np
        B, N, D, E = (8, 2048, 128, 8)
        H = 2 * D
        Bs, Ns, Ds = x.shape
        xf = x.reshape(Bs * Ns, Ds)
        logits = xf @ Wg + bg
        idx = jnp.argmax(logits, axis=-1)
        out = jnp.zeros_like(xf)
        num_experts = W1.shape[0]
        for e in range(num_experts):
            h = jax.nn.relu(xf @ W1[e] + b1[e])
            y = h @ W2[e] + b2[e]
            out = jnp.where((idx == e)[:, None], y, out)
        return out.reshape(Bs, Ns, Ds)
    h = _L0_tok_ref(x, L0_tok_W_main, L0_tok_b_main, L0_tok_W_sx, L0_tok_b_sx, L0_tok_W_sy, L0_tok_b_sy, L0_tok_ln_g, L0_tok_ln_b)
    h = h + _L0_attn_ref(_layernorm(h, axis=-1), L0_attn_A, L0_attn_B, L0_attn_C, L0_attn_D, L0_attn_Wg, L0_attn_bias_h, L0_attn_bias_y)
    h = h + _L0_ffn_ref(_layernorm(h, axis=-1), L0_ffn_W, L0_ffn_b)
    h = h + _L1_attn_ref(_layernorm(h, axis=-1), L1_attn_W_ih, L1_attn_W_hh, L1_attn_b_ih, L1_attn_b_hh, L1_attn_W_out, L1_attn_b_out)
    h = h + _L1_ffn_ref(_layernorm(h, axis=-1), L1_ffn_W1, L1_ffn_b1, L1_ffn_W2, L1_ffn_b2, L1_ffn_Wg, L1_ffn_bg)
    return h

_drawn_inputs = setup_inputs


def setup_inputs(seed=0):
    import zlib

    import numpy as np

    out = dict(_drawn_inputs(seed))
    spreads = {'L0_tok_b_main': (0.0, 0.1),
     'L0_tok_b_sx': (0.0, 0.1),
     'L0_tok_b_sy': (0.0, 0.1),
     'L0_tok_ln_g': (1.0, 0.2),
     'L0_tok_ln_b': (0.0, 0.1),
     'L0_attn_bias_h': (0.0, 0.1),
     'L0_attn_bias_y': (0.0, 0.752),
     'L1_ffn_b1': (0.0, 0.75),
     'L1_ffn_b2': (0.0, 0.1),
     'L1_ffn_bg': (0.0, 0.1)}
    factors = {'L1_attn_b_ih': 6.742, 'L1_attn_b_hh': 6.475, 'L1_attn_b_out': 2.823, 'L1_ffn_W1': 2.704}
    for name, (base, spread) in spreads.items():
        noise = np.random.default_rng([zlib.crc32(name.encode()), seed]).standard_normal(out[name].shape)
        drawn = base * np.exp(spread * noise) if base else spread * noise
        out[name] = jnp.asarray(drawn.astype(out[name].dtype))
    for name, factor in factors.items():
        out[name] = (out[name] * factor).astype(out[name].dtype)
    return out
```

```python
from contextlib import ExitStack

import concourse.bass as bass
import numpy as np
from concourse import mybir

F32 = mybir.dt.float32
BF16 = mybir.dt.bfloat16
ALU = mybir.AluOpType
ACT = mybir.ActivationFunctionType
AX = mybir.AxisListType

P = 128
B, SIDE, PATCH = 64, 14, 16
ROW = B * SIDE
HALF = ROW // 2
TILES = ROW // P
KC = 3 * PATCH * PATCH // P
PADDED = B * (SIDE + 1)
GROUP = SIDE // 2
NE = 8
EPS = 1e-5
HSCALE = float(P) ** -0.5
SPANS = ((0, 4), (4, TILES))
(V_TOKB, V_A, V_BH, V_BY, V_BIH, V_BHH, V_BO, V_B1) = (0, 1, 2, 3, 4, 6, 8, 9)
NVEC = V_B1 + 2 * NE

LOOP = (4, 10)
LINKS = 24
PLAN = [
    ["d", "o", "expert0"],
    ["ln1", "h4", "expert1"],
    ["expert2", "e"],
    ["gates", "expert3"],
    ["expert4", "z5"],
    ["expert5", "y"],
    ["expert6", "h2"],
    ["expert7", "project0", "logits"],
    ["expert8"],
    ["expert9", "z3", "onehot"],
    ["project1", "expert10"],
    ["expert11", "finish_tok"],
    ["expert12", "expert13"],
    ["expert14", "expert15", "moe_out"],
]
JOBS = {"d": (2, 1), "o": (2, -1), "h4": (2, -1), "e": (2, 1), "gates": (4, 1), "z5": (2, -1),
        "y": (2, 1), "h2": (2, 1), "project0": (1, 3), "logits": (1, -1), "z3": (2, 1),
        "onehot": (2, -1), "project1": (1, 3), "moe_out": (2, -2)}


class Row:

    def __init__(self, base, off):
        self.base, self.off, self.par = base, off, off % 2

    def valid(self):
        return not isinstance(self.base, int) or 0 <= self.base + self.off < SIDE

    def shift(self, by):
        return Row(self.base, self.off + by)

    def first(self):
        return isinstance(self.base, int) and self.base + self.off == 0

    def early(self):
        return isinstance(self.base, int) and self.base + self.off < 2

    def index(self):
        return self.base + self.off

    def count(self, per_row, n):
        return self.base * per_row + (self.off * per_row + n)

    def pair_count(self, per_row):
        if isinstance(self.base, int):
            return per_row * ((self.base + self.off) // 2 + 1)
        return self.base * (per_row // 2) + per_row * (self.off // 2 + 1)


def bank_turns():
    return [(name, j, JOBS[name][1]) for group in PLAN for name in group if name in JOBS
            for j in range(JOBS[name][0])]


TURNS = bank_turns()


def build(nc, x, w_tok, w_attn, vectors, rows_gb, w_ih, w_hh, w_out, w1, w2, w_gate, b_gate, b2,
          ident, select, out):
    with ExitStack() as ctx:
        def sb(name, shape, dt=F32):
            return ctx.enter_context(nc.sbuf_tensor(name, shape, dt))

        def psum(name):
            return ctx.enter_context(nc.psum_tensor(name, [P, 512], F32))

        def sem(name):
            return ctx.enter_context(nc.semaphore(name))

        wtok = sb("wtok", [P, KC, P])
        wattn = sb("wattn", [P, 4, P])
        vec = sb("vec", [P, NVEC])
        byscaled = sb("byscaled", [P, 1])
        a_minus_1 = sb("a_minus_1", [P, 1])
        brnn = sb("brnn", [P, 2])
        gb = sb("gb", [P, 2, P])
        wih = sb("wih", [P, 2, P])
        whh = sb("whh", [P, 2, 2, P])
        wout = sb("wout", [P, 2, P])
        w1s = sb("w1s", [P, NE, 2, P])
        w2s = sb("w2s", [P, NE, 2, P])
        wgate = sb("wgate", [P, NE])
        bgate = sb("bgate", [P, NE])
        b2s = sb("b2s", [NE, P])
        eye = sb("eye", [P, P])
        sel = sb("sel", [NE, NE, P], BF16)
        rank = sb("rank", [P, NE])
        minus_half = sb("minus_half", [P, TILES])
        zeros = sb("zeros", [P, PADDED])
        xs = [sb(f"xs{i}", [P, KC, ROW]) for i in range(2)]
        yp = [sb(f"yp{i}", [P, 1 + PADDED]) for i in range(2)]
        sh = [sb(f"sh{i}", [P, PADDED]) for i in range(2)]
        tok = [sb(f"tok{i}", [P, ROW]) for i in range(2)]
        tokT = sb("tokT", [P, TILES, P])
        h1 = sb("h1", [P, TILES, P])
        z1 = sb("z1", [P, TILES, P])
        z1f = sb("z1f", [P, ROW])
        gate = sb("gate", [P, ROW])
        inp = sb("inp", [P, ROW])
        first_term = sb("first_term", [P, B])
        hs = [sb(f"hs{i}", [P, ROW]) for i in range(2)]
        ys = sb("ys", [P, ROW])
        h2 = sb("h2", [P, TILES, P])
        h3 = [sb(f"h3_{i}", [P, TILES, P]) for i in range(2)]
        z3 = sb("z3", [P, TILES, P])
        z3f = sb("z3f", [P, ROW])
        hr = [sb(f"hr{i}", [P, 2, SIDE, B]) for i in range(2)]
        sel32 = hr[1][0:NE].rearrange("p k j b -> p (k j b)")[:, 0:NE * P]
        os_ = sb("os", [P, ROW])
        h4 = [sb(f"h4_{i}", [P, TILES, P]) for i in range(2)]
        z5 = sb("z5", [P, TILES, P])
        z5f = [sb(f"z5f{i}", [P, ROW]) for i in range(2)]
        lg = sb("lg", [P, TILES, NE])
        lmax = sb("lmax", [P, TILES])
        onehot = sb("onehot", [P, TILES, NE])
        ohf = [sb(f"ohf{i}", [NE, ROW]) for i in range(2)]
        ohb = [sb(f"ohb{i}", [NE, ROW], BF16) for i in range(2)]
        hid = sb("hid", [P, 2, HALF])
        hidm = sb("hidm", [P, 2, HALF])
        moe = sb("moe", [P, ROW])
        stats = {k: sb("stats_" + k, [P, TILES, 6]) for k in ("tok", "h1", "h2", "h4")}
        mv = {k: sb("mv_" + k, [P, TILES, 2]) for k in ("tok", "h1", "h2", "h4")}
        rstd = {k: sb("rstd_" + k, [P, TILES]) for k in ("tok", "h1", "h2", "h4", "h3")}
        veps = {k: sb("veps_" + k, [P, TILES]) for k in ("tok", "h1", "h2", "h4", "h3")}
        k2 = sb("k2", [P, TILES])
        mr = sb("mr", [P, TILES])
        s3 = sb("s3", [P, TILES])
        scratch = sb("scratch", [P, 1])

        bank = [psum("bank0"), psum("bank1")]
        rbank = [psum("rbank0"), psum("rbank1")]
        hbank = [psum("hbank0"), psum("hbank1")]
        obank = psum("obank")
        mbank = psum("mbank")

        weights_in = sem("weights_in")
        consts_done = sem("consts_done")
        x_in = [sem("x_in0"), sem("x_in1")]
        shifts_in = [sem("shifts_in0"), sem("shifts_in1")]
        stored = [sem("stored0"), sem("stored1")]
        did = {p: sem("did_" + p) for p in JOBS}
        left = {p: sem("left_" + p) for p in JOBS}
        tok_done = sem("tok_done")
        step0, step1 = sem("step0"), sem("step1")
        hid0, hid1 = sem("hid0"), sem("hid1")
        xp_done = sem("xp_done")
        e_hidden, e_mask, e_relu, e_masked, e_sum = (
            sem(n) for n in ("e_hidden", "e_mask", "e_relu", "e_masked", "e_sum"))
        moe_left = sem("moe_left")
        v = {n: sem("v_" + n) for n in ("ln1", "gates", "h2", "z3", "z5", "logits")}
        pool_done = {n: sem("pool_" + n) for n in ("tok", "h1", "affine", "h2", "h3", "h4")}
        n1_done, h1_done = sem("n1_done"), sem("h1_done")
        sig_done = sem("sig_done")
        scan_done = sem("scan_done")
        res_done = sem("res_done")
        h4_stats = sem("h4_stats")
        dve_chain = sem("dve_chain")
        scratched = sem("scratched")

        def wv(i):
            return vec[:, i:i + 1]

        def slot(eng, s, piece, before_step):
            for j, group in enumerate(PLAN):
                if s.valid():
                    before_step(s, j)
                for name in group:
                    piece(s, name)

        def all_slots(eng, piece, step, before=lambda: None, steady=lambda: None):
            for n in range(-3, LOOP[0]):
                slot(eng, Row(0, n), piece, step)
            before()
            with eng.Fori(LOOP[0], LOOP[1] - 1, 2) as base:
                for n in range(2):
                    slot(eng, Row(base, n), piece, step)
                steady()
            for n in range(LOOP[1], SIDE + 2):
                slot(eng, Row(0, n), piece, step)

        block = ctx.enter_context(nc.Block())

        @block.sync
        def _(sp):
            loads = [(wtok, w_tok), (wattn, w_attn), (vec, vectors), (gb, rows_gb), (wih, w_ih),
                     (whh, w_hh), (wout, w_out), (w1s, w1), (w2s, w2), (wgate, w_gate),
                     (bgate, b_gate), (b2s, b2), (eye, ident), (sel32, select)]
            sp.dma_start(wtok[:], w_tok).then_inc(weights_in, 16)
            for i in range(2):
                sp.dma_start(xs[i][:], x[i]).then_inc(x_in[i], 16)
            for dst, src in loads[1:]:
                sp.dma_start(dst[:] if dst is not sel32 else sel32, src).then_inc(weights_in, 16)
            sp.wait_ge(consts_done, 8)

            def piece(s, name):
                if name == "d":
                    nxt = s.shift(4)
                    if nxt.valid() and not nxt.early():
                        sp.wait_ge(did["project1"], nxt.count(1, -1))
                        sp.dma_start(xs[nxt.par][:], x[nxt.index()]).then_inc(x_in[nxt.par], 16)
                if name == "finish_tok":
                    f, nxt = s.shift(2), s.shift(3)
                    if f.valid():
                        dst, mine = sh[f.par], yp[f.par]
                        if nxt.valid():
                            sp.wait_ge(left["project1"], nxt.count(1, 1))
                        if f.first():
                            sp.dma_start(dst[112:128, :], zeros[0:16, :]).then_inc(shifts_in[0], 16)
                        s_in = shifts_in[f.par]
                        sp.dma_start(dst[64:80, 0:PADDED - 1], mine[80:96, 2:]).then_inc(s_in, 16)
                        sp.dma_start(dst[80:96, :], mine[64:80, 0:PADDED]).then_inc(s_in, 16)
                        below = yp[nxt.par][112:128, 1:] if nxt.valid() else zeros[0:16, :]
                        sp.dma_start(dst[96:112, :], below).then_inc(s_in, 16)
                        if nxt.valid():
                            if not f.first():
                                sp.wait_ge(tok_done, f.count(1, 0))
                            sp.dma_start(sh[nxt.par][112:128, :], mine[96:112, 1:])\
                                .then_inc(shifts_in[nxt.par], 16)
                if name == "moe_out":
                    q = s.shift(-2)
                    if q.valid():
                        sp.wait_ge(res_done, q.count(1, 1))
                        sp.dma_start(out[q.index()], h4[q.par][:]).then_inc(stored[0], 16)

            all_slots(sp, piece, lambda s, j: None)
            sp.wait_ge(stored[0], 16 * SIDE)

        @block.tensor
        def _(pe):
            pe.wait_ge(weights_in, 16 * 14)
            pe.wait_ge(consts_done, 8)

            def claim(s, name, job):
                t = TURNS.index((name, job, JOBS[name][1]))
                back = t - 2
                at = s
                while True:
                    if back < 0:
                        back += len(TURNS) - len(TURNS) % 2
                        if len(TURNS) % 2 and back + 1 < len(TURNS) and t % 2 == 0:
                            back = len(TURNS) - 1
                        at = at.shift(-1)
                        if isinstance(at.base, int) and at.base + at.off < -3:
                            break
                    p, j, off = TURNS[back]
                    r = at.shift(off)
                    if r.valid():
                        pe.wait_ge(left[p], r.count(JOBS[p][0], j + 1))
                        break
                    back -= 2
                return bank[t % 2]

            def transposes(s, r, name, src):
                for c, (a, b) in enumerate(SPANS):
                    dst = claim(s, name, c)
                    for m in range(a, b):
                        ins = pe.transpose(dst[:, (m - a) * P:(m - a + 1) * P], src(m), eye[:])
                    ins.then_inc(did[name], 1)

            def expert_sum(q, n):
                c, e = divmod(n, NE)
                pe.wait_ge(e_masked, q.count(16, n + 1))
                if e == 0:
                    if not (q.first() and c == 0):
                        pe.wait_ge(moe_left, q.count(2, c))
                    pe.matmul(obank[:, 0:HALF], b2s[:], ohf[q.par][:, c * HALF:(c + 1) * HALF],
                              start=True, stop=False)
                for m in range(2):
                    ins = pe.matmul(obank[:, 0:HALF], w2s[:, e, m, :], hidm[:, m, :],
                                    start=False, stop=(e == NE - 1 and m == 1))
                ins.then_inc(e_sum, 1)

            def piece(s, name):
                u, w, q, v_ = s.shift(1), s.shift(-1), s.shift(-2), s.shift(3)
                if name.startswith("project") and v_.valid():
                    c = int(name[-1])
                    dst = claim(s, name, 0)
                    if c == 0:
                        pe.wait_ge(x_in[v_.par], v_.pair_count(16))
                    for k in range(KC):
                        ins = pe.matmul(dst[:, 0:HALF], wtok[:, k, :],
                                        xs[v_.par][:, k, c * HALF:(c + 1) * HALF],
                                        start=(k == 0), stop=(k == KC - 1))
                    ins.then_inc(did[name], 1)
                if name == "d" and u.valid():
                    pe.wait_ge(tok_done, u.count(1, 1))
                    transposes(s, u, "d", lambda m: tok[u.par][:, m * P:(m + 1) * P])
                if name == "e" and u.valid():
                    pe.wait_ge(v["ln1"], u.count(1, 1))
                    transposes(s, u, "e", lambda m: z1[:, m, :])
                if name == "gates" and u.valid():
                    pe.wait_ge(left["e"], u.count(2, 2))
                    for c in range(2):
                        for i in range(2):
                            dst = claim(s, name, 2 * c + i)
                            pe.matmul(dst[:, 0:HALF], wattn[:, i, :],
                                      z1f[:, c * HALF:(c + 1) * HALF], start=True, stop=True)\
                                .then_inc(did[name], 1)
                if name == "y" and u.valid():
                    pe.wait_ge(scan_done, u.count(1, 1))
                    for c in range(2):
                        dst = claim(s, name, c)
                        pe.matmul(dst[:, 0:HALF], wattn[:, 3, :], z1f[:, c * HALF:(c + 1) * HALF],
                                  start=True, stop=False)
                        pe.matmul(dst[:, 0:HALF], wattn[:, 2, :],
                                  hs[u.par][:, c * HALF:(c + 1) * HALF],
                                  start=False, stop=True).then_inc(did[name], 1)
                if name == "h2" and u.valid():
                    pe.wait_ge(left["y"], u.count(2, 2))
                    transposes(s, u, "h2", lambda m: ys[:, m * P:(m + 1) * P])
                if name == "z3" and u.valid():
                    pe.wait_ge(v["z3"], u.count(1, 1))
                    transposes(s, u, "z3", lambda m: z3[:, m, :])
                if name == "o" and w.valid():
                    pe.wait_ge(hid0, w.count(SIDE, SIDE))
                    pe.wait_ge(hid1, w.count(SIDE, SIDE))
                    for c in range(2):
                        dst = claim(s, name, c)
                        for k in range(2):
                            states = hr[w.par][:, k, :, c * B // 2:(c + 1) * B // 2]\
                                .rearrange("p j b -> p b j")
                            ins = pe.matmul(dst[:, 0:HALF], wout[:, k, :], states,
                                            start=(k == 0), stop=(k == 1))
                        ins.then_inc(did[name], 1)
                if name == "h4" and w.valid():
                    pe.wait_ge(left["o"], w.count(2, 2))
                    transposes(s, w, "h4", lambda m: os_[:, m * P:(m + 1) * P])
                if name == "z5" and w.valid():
                    pe.wait_ge(v["z5"], w.count(1, 1))
                    transposes(s, w, "z5", lambda m: z5[:, m, :])
                if name == "logits" and w.valid():
                    pe.wait_ge(left["z5"], w.count(2, 2))
                    dst = claim(s, name, 0)
                    for m in range(TILES):
                        ins = pe.matmul(dst[:, m * NE:(m + 1) * NE],
                                        z5f[w.par][:, m * P:(m + 1) * P], wgate[:],
                                        start=True, stop=True)
                    ins.then_inc(did[name], 1)
                if name == "onehot" and w.valid():
                    pe.wait_ge(v["logits"], w.count(1, 1))
                    for c, (a, b) in enumerate(SPANS):
                        dst = claim(s, name, c)
                        for m in range(a, b):
                            ins = pe.transpose(dst[0:NE, (m - a) * P:(m - a + 1) * P],
                                               onehot[:, m, :], eye[:])
                        ins.then_inc(did[name], 1)
                if name.startswith("expert") and q.valid():
                    n = int(name[6:])
                    c, e = divmod(n, NE)
                    cols = slice(c * HALF, (c + 1) * HALF)
                    if n == 0:
                        pe.wait_ge(left["onehot"], q.count(2, 2))
                    if not (q.first() and n == 0):
                        pe.wait_ge(e_relu, q.count(16, n))
                        pe.wait_ge(e_masked, q.count(16, n))
                    pe.matmul(mbank[:, 0:HALF], sel[:, e, :], ohb[q.par][:, cols],
                              start=True, stop=True).then_inc(e_mask, 1)
                    for m in range(2):
                        ins = pe.matmul(hbank[m][:, 0:HALF], w1s[:, e, m, :], z5f[q.par][:, cols],
                                        start=True, stop=True)
                    ins.then_inc(e_hidden, 1)
                    if n > 0:
                        expert_sum(q, n - 1)
                if name == "moe_out" and q.valid():
                    expert_sum(q, 2 * NE - 1)
                    pe.wait_ge(moe_left, q.count(2, 2))
                    transposes(s, q, "moe_out", lambda m: moe[:, m * P:(m + 1) * P])

            def step(s, j):
                if j % GROUP == 0:
                    if j == 0:
                        pe.wait_ge(left["z3"], s.count(2, 2))
                    if not (s.first() and j == 0):
                        pe.wait_ge(hid0, s.count(SIDE, j))
                        pe.wait_ge(hid1, s.count(SIDE, j))
                    inputs = z3f[:].rearrange("p (b j) -> p j b", j=SIDE)[:, j:j + GROUP, :]
                    for m in range(2):
                        ins = pe.matmul(rbank[m][:, 0:HALF], wih[:, m, :], inputs,
                                        start=True, stop=False, skip_group_check=True)
                    ins.then_inc(xp_done, 1)
                at = slice((j % GROUP) * B, (j % GROUP + 1) * B)
                if s.first() and j == 0:
                    return
                prev, row = (j - 1, s) if j else (SIDE - 1, s.shift(-1))
                h = hr[row.par]
                for m in range(2):
                    for k in range(2):
                        if m == 0:
                            pe.wait_ge((hid0, hid1)[k], s.count(SIDE, j))
                        ins = pe.matmul(rbank[m][:, at], whh[:, k, m, :], h[:, k, prev, :],
                                        start=False, stop=True, skip_group_check=True)
                    ins.then_inc((step0, step1)[m], 1)

            all_slots(pe, piece, step)

        @block.scalar
        def _(act):
            act.wait_ge(weights_in, 16 * 14)
            act.wait_ge(consts_done, 8)

            def leave(r, name, job, dst, src, func=ACT.Identity, **kw):
                act.wait_ge(did[name], r.count(JOBS[name][0], job + 1))
                nc.scalar.activation(dst, src, func, **kw).then_inc(left[name], 1)

            def turn_bank(name, job):
                return bank[TURNS.index((name, job, JOBS[name][1])) % 2]

            def leave_transposes(r, name, dst):
                for c, (a, b) in enumerate(SPANS):
                    leave(r, name, c, dst(a, b), turn_bank(name, c)[:, 0:(b - a) * P])

            def piece(s, name):
                u, w, q, v_ = s.shift(1), s.shift(-1), s.shift(-2), s.shift(3)
                if name.startswith("project") and v_.valid():
                    c = int(name[-1])
                    src = turn_bank(name, 0)
                    act.wait_ge(did[name], v_.count(1, 1))
                    if c == 0 and not v_.early():
                        act.wait_ge(tok_done, v_.count(1, -1))
                        act.wait_ge(shifts_in[(v_.par + 1) % 2], v_.shift(-1).pair_count(64) - 48)
                        act.wait_ge(did["d"], v_.count(2, -2))
                    nc.scalar.activation(tok[v_.par][0:64, c * HALF:(c + 1) * HALF],
                                         src[0:64, 0:HALF], ACT.Identity, bias=vec[0:64, 0:1])
                    dst = yp[v_.par][64:128, 1:].rearrange("p (b j) -> p b j", j=SIDE + 1)[
                        :, c * B // 2:(c + 1) * B // 2, 0:SIDE]
                    nc.scalar.activation(dst, src[64:128, 0:HALF].rearrange(
                        "p (b j) -> p b j", j=SIDE), ACT.Identity).then_inc(left[name], 1)
                if name == "d" and u.valid():
                    leave_transposes(u, "d", lambda a, b: tokT[:, a:b, :])
                if name == "e" and u.valid():
                    leave_transposes(u, "e", lambda a, b: z1f[:, a * P:b * P])
                if name == "gates" and u.valid():
                    for c in range(2):
                        act.wait_ge(did["gates"], u.count(4, 2 * c + 1))
                        nc.scalar.activation(gate[:, c * HALF:(c + 1) * HALF],
                                             turn_bank("gates", 2 * c)[:, 0:HALF],
                                             ACT.Sigmoid).then_inc(sig_done, 1)
                if name == "y" and u.valid():
                    for c in range(2):
                        leave(u, "y", c, ys[:, c * HALF:(c + 1) * HALF],
                              turn_bank("y", c)[:, 0:HALF], bias=byscaled[:, 0:1], scale=HSCALE)
                if name == "z3" and u.valid():
                    if not u.first():
                        act.wait_ge(xp_done, u.count(2, 0))
                    leave_transposes(u, "z3", lambda a, b: z3f[:, a * P:b * P])
                if name == "o" and w.valid():
                    for c in range(2):
                        leave(w, "o", c, os_[:, c * HALF:(c + 1) * HALF],
                              turn_bank("o", c)[:, 0:HALF], bias=wv(V_BO))
                if name == "z5" and w.valid():
                    leave_transposes(w, "z5", lambda a, b: z5f[w.par][:, a * P:b * P])
                if name == "onehot" and w.valid():
                    for c, (a, b) in enumerate(SPANS):
                        act.wait_ge(did["onehot"], w.count(2, c + 1))
                        src = turn_bank("onehot", c)[0:NE, 0:(b - a) * P]
                        nc.scalar.activation(ohf[w.par][:, a * P:b * P], src, ACT.Identity)
                        nc.scalar.activation(ohb[w.par][:, a * P:b * P], src, ACT.Identity)\
                            .then_inc(left["onehot"], 1)
                if name.startswith("expert") and q.valid():
                    n = int(name[6:])
                    e = n % NE
                    act.wait_ge(e_hidden, q.count(16, n + 1))
                    if n >= 1 or not q.first():
                        act.wait_ge(e_masked, q.count(16, n))
                    for m in range(2):
                        ins = nc.scalar.activation(hid[:, m, :], hbank[m][:, 0:HALF],
                                                   ACT.Relu, bias=wv(V_B1 + 2 * e + m))
                    ins.then_inc(e_relu, 1)
                    if n == NE:
                        moe_half(q, 0)
                if name == "moe_out" and q.valid():
                    moe_half(q, 1)

            def moe_half(q, c):
                act.wait_ge(e_sum, q.count(16, NE * (c + 1)))
                if not q.first() and c == 0:
                    act.wait_ge(did["moe_out"], q.count(2, 0))
                nc.scalar.activation(moe[:, c * HALF:(c + 1) * HALF], obank[:, 0:HALF],
                                     ACT.Identity).then_inc(moe_left, 1)

            def step(s, j):
                if s.first() and j == 0:
                    act.wait_ge(xp_done, 1)
                else:
                    act.wait_ge(step1, s.count(SIDE, j))
                if j == 0 and not s.early():
                    act.wait_ge(did["o"], s.count(2, -2))
                at = slice((j % GROUP) * B, (j % GROUP + 1) * B)
                nc.scalar.activation(hr[s.par][:, 1, j, :], rbank[1][:, at], ACT.Relu,
                                     bias=brnn[:, 1:2]).then_inc(hid1, 1)

            all_slots(act, piece, step)

        @block.gpsimd
        def _(pool):
            def inverse_root(key, r, per_row=1):
                nc.gpsimd.tensor_tensor(rstd[key][:], veps[key][:], minus_half[:], ALU.pow)\
                    .then_inc(pool_done[key], 1)

            pool.wait_ge(consts_done, 8)

            def piece(s, name):
                u, w = s.shift(1), s.shift(-1)
                if name == "ln1" and u.valid():
                    pool.wait_ge(n1_done, u.count(3, 1))
                    inverse_root("tok", u)
                    pool.wait_ge(n1_done, u.count(3, 2))
                    g = gb[:, 0, :].unsqueeze(1).broadcast_to([P, TILES, P])
                    b = gb[:, 1, :].unsqueeze(1).broadcast_to([P, TILES, P])
                    nc.gpsimd.tensor_tensor(h1[:], h1[:], g, ALU.mult)\
                        .then_inc(pool_done["affine"], 1)
                    pool.wait_ge(pool_done["affine"], u.count(2, 1))
                    nc.gpsimd.tensor_tensor(h1[:], h1[:], b, ALU.add)\
                        .then_inc(pool_done["affine"], 1)
                    pool.wait_ge(n1_done, u.count(3, 3))
                    inverse_root("h1", u)
                if name == "h2" and u.valid():
                    pool.wait_ge(h1_done, u.count(2, 1))
                    inverse_root("h2", u)
                    pool.wait_ge(h1_done, u.count(2, 2))
                    inverse_root("h3", u)
                if name == "h4" and w.valid():
                    pool.wait_ge(h4_stats, w.count(1, 1))
                    inverse_root("h4", w)

            all_slots(pool, piece, lambda s, j: None)

        @block.vector
        def _(dve):
            links = [0]

            def link(ins, s=Row(0, 0)):
                links[0] += 1
                ins.then_inc(dve_chain, 1)
                if isinstance(s.base, int):
                    dve.wait_ge(dve_chain, links[0])
                else:
                    dve.wait_ge(dve_chain, (s.base - LOOP[0]) * LINKS + links[0])

            dve.memset(zeros[:], 0.0).then_inc(consts_done, 1)
            dve.memset(minus_half[:], -0.5).then_inc(consts_done, 1)
            for i in range(2):
                link(dve.memset(yp[i][:], 0.0))
            for e in range(NE):
                link(dve.memset(rank[:, e:e + 1], float(NE - e)))
            dve.wait_ge(weights_in, 16 * 14)
            dve.tensor_copy(sel[:].rearrange("p e f -> p (e f)"), sel32).then_inc(consts_done, 1)
            dve.tensor_scalar(byscaled[:], wv(V_BY), HSCALE, None, ALU.mult)\
                .then_inc(consts_done, 1)
            dve.tensor_scalar(a_minus_1[:], wv(V_A), -1.0, None, ALU.add).then_inc(consts_done, 1)
            dve.tensor_tensor(brnn[:], vec[:, V_BIH:V_BIH + 2], vec[:, V_BHH:V_BHH + 2], ALU.add)\
                .then_inc(consts_done, 1)
            dve.tensor_copy(k2[:], minus_half[:]).then_inc(consts_done, 1)
            dve.tensor_copy(mr[:], minus_half[:]).then_inc(consts_done, 1)
            dve.wait_ge(consts_done, 8)

            def turn_bank(name, job):
                return bank[TURNS.index((name, job, JOBS[name][1])) % 2]

            links_before = [0]

            def steady():
                turns = (LOOP[1] - LOOP[0]) // 2
                assert links[0] - links_before[0] == 2 * LINKS, links[0] - links_before[0]
                links[0] += (turns - 1) * 2 * LINKS

            def moments(s, key, src):
                for m in range(TILES):
                    ins = dve.bn_stats(stats[key][:, m, :], src[:, m, :])
                link(ins, s)
                dve.memset(scratch[:], 0.0).then_inc(scratched, 1)
                for m in range(TILES):
                    ins = dve.bn_aggr(mv[key][:, m, :], stats[key][:, m, :])
                link(ins, s)
                return dve.tensor_scalar(veps[key][:], mv[key][:, :, 1], EPS, None, ALU.add)

            def normalise(dst, src, key, scale):
                for m in range(TILES):
                    ins = dve.scalar_tensor_tensor(
                        dst[:, m, :], src[:, m, :], mv[key][:, m, 0:1],
                        scale[:, m:m + 1].broadcast_to([P, P]), ALU.subtract, ALU.mult)
                return ins

            def piece(s, name):
                u, w, q, v_, f = s.shift(1), s.shift(-1), s.shift(-2), s.shift(3), s.shift(2)
                if name == "finish_tok" and f.valid():
                    dve.wait_ge(shifts_in[f.par], f.pair_count(64))
                    dve.wait_ge(left["project1"], f.count(1, 1))
                    if not f.early():
                        dve.wait_ge(did["d"], f.count(2, -2))
                    own = yp[f.par][64:128, 1:].rearrange("p (b j) -> p b j", j=SIDE + 1)
                    other = sh[f.par][64:128, :].rearrange("p (b j) -> p b j", j=SIDE + 1)
                    dve.scalar_tensor_tensor(
                        tok[f.par][64:128, :].rearrange("p (b j) -> p b j", j=SIDE),
                        own[:, :, 0:SIDE], vec[64:128, 0:1], other[:, :, 0:SIDE],
                        ALU.add, ALU.add).then_inc(tok_done, 1)
                if name == "ln1" and u.valid():
                    dve.wait_ge(left["d"], u.count(2, 2))
                    moments(s, "tok", tokT).then_inc(n1_done, 1)
                    dve.wait_ge(pool_done["tok"], u.count(1, 1))
                    normalise(h1, tokT, "tok", rstd["tok"]).then_inc(n1_done, 1)
                    dve.wait_ge(pool_done["affine"], u.count(2, 2))
                    moments(s, "h1", h1).then_inc(n1_done, 1)
                    dve.wait_ge(pool_done["h1"], u.count(1, 1))
                    if not u.first():
                        dve.wait_ge(did["e"], u.count(2, 0))
                    normalise(z1, h1, "h1", rstd["h1"]).then_inc(v["ln1"], 1)
                if name == "gates" and u.valid():
                    for c in range(2):
                        cols = slice(c * HALF, (c + 1) * HALF)
                        dve.wait_ge(sig_done, u.count(2, c + 1))
                        link(dve.tensor_scalar(gate[:, cols], gate[:, cols], 0.05, 0.95,
                                               ALU.max, ALU.min), s)
                        dve.sem_inc(left["gates"], 1)
                        dve.wait_ge(did["gates"], u.count(4, 2 * c + 2))
                        dve.scalar_tensor_tensor(inp[:, cols], turn_bank("gates", 2 * c + 1)[:, 0:HALF],
                                                 wv(V_BH), gate[:, cols], ALU.add, ALU.mult)\
                            .then_inc(left["gates"], 1)
                    dve.wait_ge(left["gates"], u.count(4, 4))
                    link(dve.tensor_scalar(gate[:], gate[:], a_minus_1[:, 0:1], 1.0,
                                           ALU.mult, ALU.add), s)
                    a3 = gate[:].rearrange("p (b j) -> p b j", j=SIDE)
                    b3 = inp[:].rearrange("p (b j) -> p b j", j=SIDE)
                    if not u.first():
                        before = hs[1 - u.par][:].rearrange("p (b j) -> p b j", j=SIDE)
                        link(dve.tensor_tensor(first_term[:], a3[:, :, 0], before[:, :, SIDE - 1],
                                               ALU.mult), s)
                        link(dve.tensor_tensor(b3[:, :, 0], b3[:, :, 0], first_term[:], ALU.add), s)
                    link(dve.memset(a3[:, :, 0], 0.0), s)
                    if not u.early():
                        dve.wait_ge(did["y"], u.count(2, -2))
                    dve.tensor_tensor_scan(hs[u.par][:], gate[:], inp[:], 0.0, ALU.mult, ALU.add)\
                        .then_inc(scan_done, 1)
                    dve.wait_ge(scan_done, u.count(1, 1))
                if name == "h2" and u.valid():
                    for c, (a, b) in enumerate(SPANS):
                        dve.wait_ge(did["h2"], u.count(2, c + 1))
                        dve.tensor_tensor(h2[:, a:b, :], h1[:, a:b, :],
                                          turn_bank("h2", c)[:, 0:(b - a) * P].rearrange(
                                              "p (m f) -> p m f", f=P), ALU.add)\
                            .then_inc(left["h2"], 1)
                    dve.wait_ge(left["h2"], u.count(2, 2))
                    moments(s, "h2", h2).then_inc(h1_done, 1)
                    dve.wait_ge(pool_done["h2"], u.count(1, 1))
                    r2, m2, v2 = rstd["h2"], mv["h2"][:, :, 0], mv["h2"][:, :, 1]
                    link(dve.tensor_scalar(k2[:], r2[:], 1.0, None, ALU.add), s)
                    link(dve.tensor_tensor(mr[:], k2[:], k2[:], ALU.mult), s)
                    link(dve.tensor_tensor(mr[:], mr[:], v2, ALU.mult), s)
                    dve.tensor_scalar(veps["h3"][:], mr[:], EPS, None, ALU.add)\
                        .then_inc(h1_done, 1)
                    dve.wait_ge(pool_done["h3"], u.count(1, 1))
                    link(dve.tensor_tensor(s3[:], k2[:], rstd["h3"][:], ALU.mult), s)
                    if not u.first():
                        dve.wait_ge(did["z3"], u.count(2, 0))
                    normalise(z3, h2, "h2", s3).then_inc(v["z3"], 1)
                    dst = h3[u.par]
                    link(normalise(dst, h2, "h2", r2), s)
                    dve.tensor_tensor(dst[:], dst[:], h2[:], ALU.add).then_inc(v["h2"], 1)
                    dve.wait_ge(v["h2"], u.count(1, 1))
                if name == "h4" and w.valid():
                    if not w.early():
                        dve.wait_ge(stored[0], w.count(16, -16))
                    for c, (a, b) in enumerate(SPANS):
                        dve.wait_ge(did["h4"], w.count(2, c + 1))
                        dve.tensor_tensor(h4[w.par][:, a:b, :], h3[w.par][:, a:b, :],
                                          turn_bank("h4", c)[:, 0:(b - a) * P].rearrange(
                                              "p (m f) -> p m f", f=P), ALU.add)\
                            .then_inc(left["h4"], 1)
                    dve.wait_ge(left["h4"], w.count(2, 2))
                    moments(s, "h4", h4[w.par]).then_inc(h4_stats, 1)
                    dve.wait_ge(pool_done["h4"], w.count(1, 1))
                    if not w.first():
                        dve.wait_ge(did["z5"], w.count(2, 0))
                    normalise(z5, h4[w.par], "h4", rstd["h4"]).then_inc(v["z5"], 1)
                if name == "logits" and w.valid():
                    dve.wait_ge(did["logits"], w.count(1, 1))
                    lg_in = turn_bank("logits", 0)[:, 0:TILES * NE].rearrange(
                        "p (m e) -> p m e", e=NE)
                    dve.tensor_tensor(lg[:], lg_in, bgate[:].unsqueeze(1).broadcast_to(
                        [P, TILES, NE]), ALU.add).then_inc(left["logits"], 1)
                    dve.wait_ge(left["logits"], w.count(1, 1))
                    link(dve.tensor_reduce(lmax[:], lg[:], AX.X, ALU.max), s)
                    link(dve.tensor_tensor(lg[:], lg[:], lmax[:].unsqueeze(2).broadcast_to(
                        [P, TILES, NE]), ALU.is_equal), s)
                    link(dve.tensor_tensor(lg[:], lg[:], rank[:].unsqueeze(1).broadcast_to(
                        [P, TILES, NE]), ALU.mult), s)
                    link(dve.tensor_reduce(lmax[:], lg[:], AX.X, ALU.max), s)
                    if not w.first():
                        dve.wait_ge(did["onehot"], w.count(2, 0))
                    link(dve.tensor_tensor(onehot[:], lmax[:].unsqueeze(2).broadcast_to(
                        [P, TILES, NE]), rank[:].unsqueeze(1).broadcast_to([P, TILES, NE]),
                        ALU.is_equal), s)
                    dve.sem_inc(v["logits"], 1)
                if name.startswith("expert") and q.valid():
                    n = int(name[6:])
                    dve.wait_ge(e_relu, q.count(16, n + 1))
                    dve.wait_ge(e_mask, q.count(16, n + 1))
                    if n >= 1 or not q.first():
                        dve.wait_ge(e_sum, q.count(16, n))
                    dve.tensor_tensor(hidm[:], hid[:],
                                      mbank[:, 0:HALF].unsqueeze(1).broadcast_to([P, 2, HALF]),
                                      ALU.mult).then_inc(e_masked, 1)
                if name == "moe_out" and q.valid():
                    for c, (a, b) in enumerate(SPANS):
                        dve.wait_ge(did["moe_out"], q.count(2, c + 1))
                        ins = dve.tensor_tensor(h4[q.par][:, a:b, :], h4[q.par][:, a:b, :],
                                                turn_bank("moe_out", c)[:, 0:(b - a) * P].rearrange(
                                                    "p (m f) -> p m f", f=P), ALU.add)\
                            .then_inc(left["moe_out"], 1)
                    dve.wait_ge(left["moe_out"], q.count(2, 2))
                    dve.sem_inc(res_done, 1)

            def step(s, j):
                if s.first() and j == 0:
                    dve.wait_ge(xp_done, 1)
                else:
                    dve.wait_ge(step0, s.count(SIDE, j))
                if j == 0 and not s.early():
                    dve.wait_ge(did["o"], s.count(2, -2))
                at = slice((j % GROUP) * B, (j % GROUP + 1) * B)
                dve.tensor_scalar(hr[s.par][:, 0, j, :], rbank[0][:, at], brnn[:, 0:1], 0.0,
                                  ALU.add, ALU.max).then_inc(hid0, 1)

            all_slots(dve, piece, step, lambda: links_before.append(links_before.pop() + links[0]), steady)


def patch_rows(x):
    t = np.asarray(x).reshape(B, 3, SIDE, PATCH, SIDE, PATCH).transpose(2, 1, 3, 5, 0, 4)
    return np.ascontiguousarray(t.reshape(SIDE, KC, P, ROW).transpose(0, 2, 1, 3))


def patch_weights(w_main, w_sx, w_sy):
    d, ds, h = w_main.shape[0], w_sx.shape[0], PATCH // 2
    w = np.zeros((d + 4 * ds, 3, PATCH, PATCH), w_main.dtype)
    w[:d] = w_main.reshape(d, 3, PATCH, PATCH)
    sx, sy = (a.reshape(ds, 3, PATCH, PATCH) for a in (w_sx, w_sy))
    w[d:d + ds, :, :, h:] = sx[:, :, :, :h]
    w[d + ds:d + 2 * ds, :, :, :h] = sx[:, :, :, h:]
    w[d + 2 * ds:d + 3 * ds, :, h:, :] = sy[:, :, :h, :]
    w[d + 3 * ds:, :, :h, :] = sy[:, :, h:, :]
    return np.ascontiguousarray(w.reshape(-1, KC, P).transpose(2, 1, 0))


def kernel(**inputs):
    import concourse.bacc as bacc
    from concourse.bass_utils import run_bass_kernel_spmd

    a = {k: np.asarray(t) for k, t in inputs.items()}
    f = a["x"].dtype
    tok, at, rn, ff = "L0_tok_", "L0_attn_", "L1_attn_", "L1_ffn_"
    columns = [np.concatenate([a[tok + "b_main"], a[tok + "b_sx"], a[tok + "b_sx"],
                               a[tok + "b_sy"], a[tok + "b_sy"]]),
               a[at + "A"], a[at + "bias_h"], a[at + "bias_y"],
               a[rn + "b_ih"][:P], a[rn + "b_ih"][P:], a[rn + "b_hh"][:P], a[rn + "b_hh"][P:],
               a[rn + "b_out"], *a[ff + "b1"].reshape(2 * NE, P)]
    arrays = {
        "x": patch_rows(a["x"]),
        "w_tok": patch_weights(a[tok + "W_main"], a[tok + "W_sx"], a[tok + "W_sy"]),
        "w_attn": np.stack([a[at + n].T for n in ("Wg", "B", "C", "D")], 1),
        "vectors": np.stack(columns, 1),
        "rows_gb": np.broadcast_to(np.stack([a[tok + "ln_g"], a[tok + "ln_b"]]), (P, 2, P)),
        "w_ih": a[rn + "W_ih"].reshape(2, P, P).transpose(2, 0, 1),
        "w_hh": a[rn + "W_hh"].reshape(2, P, 2, P).transpose(3, 2, 0, 1),
        "w_out": a[rn + "W_out"].reshape(P, 2, P).transpose(2, 1, 0),
        "w1": a[ff + "W1"].reshape(NE, P, 2, P).transpose(1, 0, 2, 3),
        "w2": a[ff + "W2"].reshape(NE, 2, P, P).transpose(2, 0, 1, 3),
        "w_gate": a[ff + "Wg"],
        "b_gate": np.broadcast_to(a[ff + "bg"], (P, NE)),
        "b2": a[ff + "b2"],
        "ident": np.eye(P, dtype=f),
        "select": np.repeat(np.eye(NE, dtype=f)[:, :, None], P, 2).reshape(NE, NE * P),
    }
    arrays = {k: np.ascontiguousarray(t) for k, t in arrays.items()}
    nc = bacc.Bacc("TRN2", target_bir_lowering=False, num_devices=1)
    args = [nc.dram_tensor(f"in_{k}", t.shape, mybir.dt.from_np(t.dtype),
                           kind="ExternalInput").ap() for k, t in arrays.items()]
    out = nc.dram_tensor("out", (SIDE, P, TILES, P), F32, kind="ExternalOutput").ap()
    build(nc, *args, out)
    r = run_bass_kernel_spmd(nc, [{f"in_{k}": t for k, t in arrays.items()}], core_ids=[0])
    got = np.asarray(r.results[0]["out"])
    got = got.transpose(0, 2, 1, 3).reshape(SIDE, B, SIDE, P).transpose(1, 0, 2, 3)
    return np.ascontiguousarray(got.reshape(B, SIDE * SIDE, P))
```

```python
from contextlib import ExitStack

import concourse.bass as bass
import numpy as np
from concourse import mybir

F32 = mybir.dt.float32
BF16 = mybir.dt.bfloat16
U32 = mybir.dt.uint32
I32 = mybir.dt.int32
ALU = mybir.AluOpType
ACT = mybir.ActivationFunctionType
AX = mybir.AxisListType

P = 128
B, SIDE, PATCH = 64, 14, 16
ROW = B * SIDE
HALF = ROW // 2
TILES = ROW // P
KC = 3 * PATCH * PATCH // P
PADDED = B * (SIDE + 1)
GROUP = 4
NE = 8
TOKENS = SIDE * ROW
TS = 256
MT = TS // P
CAP = TOKENS + TS
NTILES = (TOKENS + NE * (TS - 1)) // TS
WIDE = 2 * P + 4
WEXP = 4 * P + 4
NBUF = 8
NFIN = 4
NOWHERE = 60000.0
EPS = 1e-5
HSCALE = float(P) ** -0.5
SPANS = ((0, 4), (4, TILES))
V_TOKB, V_A, V_BH, V_BY, V_BO, NVEC = range(6)

LOOP = (2, 8)
LINKS = 21
POOL_LINKS = 10
PLAN = [
    ["e", "xp1", "d"],
    ["gates0", "tok_stats", "o0"],
    ["open0", "gates1"],
    ["open1", "o1", "n1", "project0a"],
    ["scan", "h4", "project0b"],
    ["h4_add", "y0", "y1", "h3n"],
    ["h1_stats", "h2", "keep0"],
    ["h2_add", "h4_stats", "xp2", "keep1", "z1n", "project0c", "project1a"],
    ["h2_stats", "xp3", "z5n", "project1b"],
    ["project1c"],
    ["z5", "z3n"],
    ["logits"],
    ["keep2", "finish_tok", "pick", "z3"],
    ["keep3", "xp0", "prefix", "place"],
]
JOBS = {"e": (("e", 0), ("e", 1), 1), "gates0": (("sigmoid", 0), ("inputs", 0), 1),
        "gates1": (("sigmoid", 1), ("inputs", 1), 1), "o0": (("o", 0), -1), "o1": (("o", 1), -1),
        "h4": (("h4", 0), ("h4", 1), -1), "y0": (("y", 0), 1), "y1": (("y", 1), 1),
        "h2": (("h2", 0), ("h2", 1), 1), "d": (("d", 0), ("d", 1), 2),
        "z5": (("z5", 0), ("z5", 1), -1), "logits": (("logits", 0), -1),
        "z3": (("z3", 0), ("z3", 1), 1), "prefix": (("prefix", 0), -1)}
PER_ROW = {"e": 2, "sigmoid": 2, "inputs": 2, "o": 2, "h4": 2, "y": 2, "h2": 2, "d": 2, "z5": 2,
           "logits": 1, "z3": 2, "prefix": 1, "project0": 1, "project1": 1}
GENERAL = 4


class Row:

    def __init__(self, base, off):
        self.base, self.off, self.par = base, off, off % 2

    def valid(self):
        return not isinstance(self.base, int) or 0 <= self.base + self.off < SIDE

    def shift(self, by):
        return Row(self.base, self.off + by)

    def first(self):
        return isinstance(self.base, int) and self.base + self.off == 0

    def early(self):
        return isinstance(self.base, int) and self.base + self.off < 2

    def index(self):
        return self.base + self.off

    def count(self, per_row, n):
        return self.base * per_row + (self.off * per_row + n)

    def pair_count(self, per_row):
        if isinstance(self.base, int):
            return per_row * ((self.base + self.off) // 2 + 1)
        return self.base * (per_row // 2) + per_row * (self.off // 2 + 1)


def bank_turns():
    turns = []
    for name in (name for group in PLAN for name in group if name in JOBS):
        *jobs, off = JOBS[name]
        turns += [(kind, number, off) for kind, number in jobs]
    return turns


def bank_of(kind, job):
    return [t[:2] for t in TURNS].index((kind, job)) % GENERAL


TURNS = bank_turns()


def steps_of(group):
    first = group // 2 * 2 * GROUP
    return range(first + group % 2, min(SIDE, first + 2 * GROUP), 2)


def build(nc, x, w_tok, w_attn, vectors, rows_gb, w_ih, w_hh, w_out, b_rnn, w_gate, b_gate,
          ident, first_ids, triangle, experts, places, out):
    with ExitStack() as ctx:
        def sb(name, shape, dt=F32):
            return ctx.enter_context(nc.sbuf_tensor(name, shape, dt))

        def psum(name):
            return ctx.enter_context(nc.psum_tensor(name, [P, 512], F32))

        def sem(name):
            return ctx.enter_context(nc.semaphore(name))

        wtok = sb("wtok", [P, KC, P])
        wattn = sb("wattn", [P, 4, P])
        vec = sb("vec", [P, NVEC])
        byscaled = sb("byscaled", [P, 1])
        a_minus_1 = sb("a_minus_1", [P, 1])
        brow = sb("brow", [1, 2, 2 * P])
        bsplit = sb("bsplit", [1, 3, 2 * P], BF16)
        bparts = sb("bparts", [3, 2 * P], BF16)
        ones3 = sb("ones3", [3, GROUP * B], BF16)
        gb = sb("gb", [P, 2, P])
        wih = sb("wih", [P, 2, P])
        whh = sb("whh", [P, 2, 2, P])
        whhp = [sb(f"whhp{i}", [P, 2, 2, P], BF16) for i in range(3)]
        wout = sb("wout", [P, 2, P])
        wgate = sb("wgate", [P, NE])
        bgate = sb("bgate", [P, NE])
        eye = sb("eye", [P, P])
        tri32 = sb("tri32", [P, P])
        tri = sb("tri", [P, P], BF16)
        ones = sb("ones", [P, P], BF16)
        region = sb("region", [P, NE])
        free = sb("free", [P, NE])
        ids = sb("ids", [P, TILES])
        rank = sb("rank", [P, NE])
        minus_half = sb("minus_half", [P, TILES])
        zeros = sb("zeros", [P, PADDED])
        xs = [sb(f"xs{i}", [P, KC, ROW]) for i in range(2)]
        yp = [sb(f"yp{i}", [P, 1 + PADDED]) for i in range(2)]
        sh = [sb(f"sh{i}", [P, PADDED]) for i in range(2)]
        tok = [sb(f"tok{i}", [P, ROW]) for i in range(2)]
        tokT = sb("tokT", [P, TILES, P])
        h1 = [sb(f"h1_{i}", [P, TILES, P]) for i in range(2)]
        z1 = sb("z1", [P, TILES, P])
        z1f = sb("z1f", [P, ROW])
        gate = sb("gate", [P, ROW])
        inp = sb("inp", [P, ROW])
        decay = sb("decay", [P, ROW])
        first_term = sb("first_term", [P, B])
        hs = [sb(f"hs{i}", [P, ROW]) for i in range(2)]
        ys = sb("ys", [P, ROW])
        h2 = sb("h2", [P, TILES, P])
        h3 = [sb(f"h3_{i}", [P, TILES, P]) for i in range(2)]
        z3 = sb("z3", [P, TILES, P])
        z3f = sb("z3f", [P, ROW])
        hr = [sb(f"hr{i}", [P, SIDE, 2, B]) for i in range(2)]
        hparts = [sb(f"hparts{i}", [P, 3, 2, B], BF16) for i in range(2)]
        rest = sb("rest", [P, 2, B])
        os_ = sb("os", [P, ROW])
        zh = [sb(f"zh{i}", [P, TILES, WIDE]) for i in range(2)]
        z5f = sb("z5f", [P, ROW])
        lg = sb("lg", [P, TILES, NE])
        lmax = sb("lmax", [P, TILES])
        onehot = sb("onehot", [P, TILES, NE])
        onehotb = sb("onehotb", [P, TILES * NE], BF16)
        place = sb("place", [P, TILES, NE])
        placef = sb("placef", [P, TILES])
        placeu = [sb(f"placeu{i}", [P, TILES], U32) for i in range(2)]
        pad = sb("pad", [P, MT, WIDE])
        tilex = sb("tilex", [1, NTILES, NE])
        tab = {n: t[0:1, 0:NTILES * NE].rearrange("p (t e) -> p t e", e=NE)
               for n, t in (("a", gate), ("b", inp))}
        row8 = {n: sb("row8_" + n, [1, NE]) for n in ("count", "tiles", "ends", "starts", "one")}
        row8i = sb("row8i", [1, NE], I32)
        tilef = {n: sb("tilef_" + n, [1, NTILES]) for n in ("place", "expert", "any")}
        tileu = {n: sb("tileu_" + n, [1, NTILES], U32) for n in ("place", "expert")}
        freeu = sb("freeu", [1, NE], U32)
        flat = [xs[i][:].rearrange("p k n -> p (k n)") for i in range(2)]
        rows = [flat[0][:, i * MT * WIDE:(i + 1) * MT * WIDE].rearrange("p (m f) -> p m f", f=WIDE)
                for i in range(NBUF)]
        wexp = [flat[1][:, i * WEXP:(i + 1) * WEXP] for i in range(NBUF)]
        after = NBUF * MT * WIDE
        fin = [flat[0][:, after + i * TS:after + (i + 1) * TS].rearrange("p (m f) -> p m f", f=P)
               for i in range(NFIN)]
        after = NBUF * WEXP
        hid = [flat[1][:, after + i * 2 * TS:after + (i + 1) * 2 * TS].rearrange(
            "p (m f) -> p m f", m=2) for i in range(2)]
        zt = [z1f[:, i * TS:(i + 1) * TS] for i in range(2)]
        yt = [ys[:, i * TS:(i + 1) * TS] for i in range(2)]
        fid = [sb(f"fid{i}", [P, MT], U32) for i in range(NFIN)]
        stats = {k: sb("stats_" + k, [P, TILES, 6]) for k in ("tok", "h1", "h2", "h4")}
        mv = {k: sb("mv_" + k, [P, TILES, 2]) for k in ("tok", "h1", "h2", "h4")}
        veps = {k: sb("veps_" + k, [P, TILES]) for k in ("tok", "h1", "h2", "h4", "h3")}
        minus_mean = {k: sb("minus_mean_" + k, [P, TILES]) for k in ("tok", "h1", "h2", "h4")}
        scale = {k: sb("scale_" + k, [P, TILES]) for k in ("tok", "h1", "h2", "h4", "h3")}
        shift = {k: sb("shift_" + k, [P, TILES]) for k in ("tok", "h1", "h2", "h4", "h3")}
        rstd = {k: sb("rstd_" + k, [P, TILES]) for k in ("h2", "h3")}
        one7, eps7 = sb("one7", [P, TILES]), sb("eps7", [P, TILES])
        scratch = sb("scratch", [P, 1])
        carrier = sb("carrier", [P, 3])

        bank = [psum(f"bank{i}") for i in range(GENERAL)]
        pbank = [psum(f"pbank{i}") for i in range(2)]
        rbank = [psum(f"rbank{i}") for i in range(2)]
        wtok_in = sem("wtok_in")
        weights_in = sem("weights_in")
        zeroed = sem("zeroed")
        consts_done = sem("consts_done")
        x_in = [sem("x_in0"), sem("x_in1")]
        shifts_in = [sem("shifts_in0"), sem("shifts_in1")]
        did = {p: sem("did_" + p) for p in PER_ROW}
        left = {p: sem("left_" + p) for p in PER_ROW}
        tok_done = sem("tok_done")
        stepped = sem("stepped")
        part_done = [sem(f"part_done{i}") for i in range(3)]
        rest_done = sem("rest_done")
        kept = sem("kept")
        clipped, decayed = sem("clipped"), sem("decayed")
        split_done = sem("split_done")
        bparts_in = sem("bparts_in")
        xp_done = sem("xp_done")
        v = {n: sem("v_" + n) for n in ("logits", "place")}
        moments_done = {k: sem("moments_" + k) for k in ("tok", "h1", "h2", "h4")}
        scaled = {k: sem("scaled_" + k) for k in ("tok", "h1", "h2", "h4")}
        affine = sem("affine")
        n1_done, z1_done, z3_done, h3_done, z5_done = (
            sem(n + "_done") for n in ("n1", "z1", "z3", "h3", "z5"))
        scattered = [sem("scattered0"), sem("scattered1")]
        ends_known, tables_done, pads_in = sem("ends_known"), sem("tables_done"), sem("pads_in")
        tile_in = [sem(f"tile_in{i}") for i in range(NBUF)]
        t_z, t_zt, t_h, t_hid, t_hid1, t_y, t_yt, t_o, t_fin = (
            sem("t_" + n) for n in ("z", "zt", "h", "hid", "hid1", "y", "yt", "o", "fin"))
        out_done = [sem(f"out_done{i}") for i in range(NFIN)]
        scan_done = sem("scan_done")
        dve_chain, pool_chain = sem("dve_chain"), sem("pool_chain")
        t_ids = sem("t_ids")
        t_carried = sem("t_carried")
        scratched = sem("scratched")
        carried = sem("carried")

        def wv(i):
            return vec[:, i:i + 1]

        def slot(eng, s, piece, before_step):
            for j, group in enumerate(PLAN):
                if s.valid():
                    before_step(s, j)
                for name in group:
                    piece(s, name)

        def all_slots(eng, piece, step, before=lambda: None, steady=lambda: None):
            for n in range(-4, LOOP[0] + 1):
                slot(eng, Row(0, n), piece, step)
            before()
            with eng.Fori(LOOP[0], LOOP[1] - 1, 2) as base:
                for n in range(2):
                    slot(eng, Row(base, n + 1), piece, step)
                steady()
            for n in range(LOOP[1] + 1, SIDE + 1):
                slot(eng, Row(0, n), piece, step)

        def write_pads(eng, some):
            eng.wait_ge(ends_known, 1)
            for e in some:
                at = eng.value_load(freeu[0:1, e:e + 1], min_val=0, max_val=NE * CAP - TS)
                eng.dma_start(places[bass.ds(at, TS), :].rearrange("(p m) f -> p m f", m=MT),
                              pad[:]).then_inc(pads_in, 16)

        block = ctx.enter_context(nc.Block())

        @block.sync
        def _(sp):
            sp.dma_start(wtok[:], w_tok).then_inc(wtok_in, 16)
            sp.dma_start(xs[0][:], x[0]).then_inc(x_in[0], 16)
            for dst, src in [(wattn, w_attn), (vec, vectors), (gb, rows_gb), (wih, w_ih),
                             (whh, w_hh), (wout, w_out), (brow, b_rnn), (wgate, w_gate),
                             (bgate, b_gate), (eye, ident), (ids, first_ids), (tri32, triangle)]:
                sp.dma_start(dst[:], src).then_inc(weights_in, 16)
            sp.dma_start(xs[1][:], x[1]).then_inc(x_in[1], 16)
            sp.wait_ge(split_done, 1)
            for i in range(3):
                sp.dma_start(bparts[i:i + 1, :], bsplit[0:1, i, :]).then_inc(bparts_in, 16)
            sp.wait_ge(consts_done, 1)

            def piece(s, name):
                if name == "xp1":
                    nxt = s.shift(5)
                    if nxt.valid() and not nxt.early():
                        sp.wait_ge(did["project1"], nxt.count(1, -1))
                        sp.dma_start(xs[nxt.par][:], x[nxt.index()]).then_inc(x_in[nxt.par], 16)
                if name == "finish_tok":
                    f, nxt = s.shift(3), s.shift(4)
                    if f.valid():
                        dst, mine = sh[f.par], yp[f.par]
                        if nxt.valid():
                            sp.wait_ge(left["project1"], nxt.count(1, 1))
                        if f.first():
                            sp.dma_start(dst[112:128, :], zeros[0:16, :]).then_inc(shifts_in[0], 16)
                        s_in = shifts_in[f.par]
                        sp.dma_start(dst[64:80, 0:PADDED - 1], mine[80:96, 2:]).then_inc(s_in, 16)
                        sp.dma_start(dst[80:96, :], mine[64:80, 0:PADDED]).then_inc(s_in, 16)
                        below = yp[nxt.par][112:128, 1:] if nxt.valid() else zeros[0:16, :]
                        sp.dma_start(dst[96:112, :], below).then_inc(s_in, 16)
                        if nxt.valid():
                            if not f.first():
                                sp.wait_ge(tok_done, f.count(1, 0))
                            sp.dma_start(sh[nxt.par][112:128, :], mine[96:112, 1:])\
                                .then_inc(shifts_in[nxt.par], 16)
            all_slots(sp, piece, lambda s, j: None)

            write_pads(sp, range(0, NE, 2))
            sp.wait_ge(pads_in, 16 * NE)
            for i in range(2):
                sp.wait_ge(scattered[i], 16 * TILES * SIDE // 2)
            sp.wait_ge(tables_done, 1)

            def load(t, i, first):
                if not first:
                    sp.wait_ge(t_fin, t - NBUF + 1)
                at = sp.value_load(tileu["place"][0:1, bass.ds(t, 1)], min_val=0,
                                   max_val=NE * CAP - TS)
                sp.dma_start(rows[i][:], places[bass.ds(at, TS), :].rearrange(
                    "(p m) f -> p m f", m=MT)).then_inc(tile_in[i], 16)
                e = sp.value_load(tileu["expert"][0:1, bass.ds(t, 1)], min_val=0, max_val=NE - 1)
                sp.dma_start(wexp[i][:], experts[bass.ds(e, 1), :, :].rearrange(
                    "e p w -> (e p) w")).then_inc(tile_in[i], 16)

            for i in range(NBUF):
                load(i, i, True)
            with sp.Fori(NBUF, NTILES - NBUF + 1, NBUF) as t:
                for i in range(NBUF):
                    load(t + i, i, False)

        @block.tensor
        def _(pe):
            pe.wait_ge(wtok_in, 16)

            def claim(s, name, job):
                t = [turn[:2] for turn in TURNS].index((name, job))
                before = [(s, b) for b in range(t - GENERAL, -1, -GENERAL)]
                before += [(s.shift(-1), b) for b in reversed(range(len(TURNS)))
                           if b % GENERAL == t % GENERAL]
                for at, b in before:
                    p, j, off = TURNS[b]
                    if at.shift(off).valid():
                        pe.wait_ge(left[p], at.shift(off).count(PER_ROW[p], j + 1))
                        break
                return bank[t % GENERAL]

            def transposes(s, r, name, src):
                for c, (a, b) in enumerate(SPANS):
                    dst = claim(s, name, c)
                    for m in range(a, b):
                        ins = pe.transpose(dst[:, (m - a) * P:(m - a + 1) * P], src(m), eye[:])
                    ins.then_inc(did[name], 1)

            def piece(s, name):
                u, w, v_, d = s.shift(1), s.shift(-1), s.shift(4), s.shift(2)
                if name.startswith("project") and v_.valid():
                    c, part = int(name[7]), "abc".index(name[8])
                    if part == 0 and not v_.first():
                        pe.wait_ge(left[name[:8]], v_.count(1, 0))
                    if part == 0 and c == 0:
                        pe.wait_ge(x_in[v_.par], v_.pair_count(16))
                    for k in range(part * KC // 3, (part + 1) * KC // 3):
                        ins = pe.matmul(pbank[c][:, 0:HALF], wtok[:, k, :],
                                        xs[v_.par][:, k, c * HALF:(c + 1) * HALF],
                                        start=(k == 0), stop=(k == KC - 1))
                    if part == 2:
                        ins.then_inc(did[name[:8]], 1)
                if name == "d" and d.valid():
                    if d.first():
                        pe.wait_ge(weights_in, 16 * 12)
                        pe.wait_ge(consts_done, 1)
                        pe.wait_ge(bparts_in, 48)
                    pe.wait_ge(tok_done, d.count(1, 1))
                    transposes(s, d, "d", lambda m: tok[d.par][:, m * P:(m + 1) * P])
                if name.startswith("xp"):
                    inputs_of_group(s if name != "xp0" else u, int(name[2]))
                if name == "e" and u.valid():
                    pe.wait_ge(z1_done, u.count(1, 1))
                    transposes(s, u, "e", lambda m: z1[:, m, :])
                if name in ("gates0", "gates1") and u.valid():
                    c = int(name[5])
                    pe.wait_ge(left["e"], u.count(2, 2))
                    for i, kind in enumerate(("sigmoid", "inputs")):
                        dst = claim(s, kind, c)
                        pe.matmul(dst[:, 0:HALF], wattn[:, i, :],
                                  z1f[:, c * HALF:(c + 1) * HALF], start=True, stop=True)\
                            .then_inc(did[kind], 1)
                if name in ("y0", "y1") and u.valid():
                    c = int(name[1])
                    dst = claim(s, "y", c)
                    pe.matmul(dst[:, 0:HALF], wattn[:, 3, :], z1f[:, c * HALF:(c + 1) * HALF],
                              start=True, stop=False)
                    if c == 0:
                        pe.wait_ge(scan_done, u.count(1, 1))
                    pe.matmul(dst[:, 0:HALF], wattn[:, 2, :],
                              hs[u.par][:, c * HALF:(c + 1) * HALF],
                              start=False, stop=True).then_inc(did["y"], 1)
                if name == "h2" and u.valid():
                    pe.wait_ge(left["y"], u.count(2, 2))
                    transposes(s, u, "h2", lambda m: ys[:, m * P:(m + 1) * P])
                if name == "z3" and u.valid():
                    pe.wait_ge(z3_done, u.count(1, 1))
                    transposes(s, u, "z3", lambda m: z3[:, m, :])
                if name in ("o0", "o1") and w.valid():
                    c = int(name[1])
                    pe.wait_ge(kept, w.count(4, 4))
                    dst = claim(s, "o", c)
                    for k in range(2):
                        states = hr[w.par][:, :, k, c * B // 2:(c + 1) * B // 2]\
                            .rearrange("p j b -> p b j")
                        ins = pe.matmul(dst[:, 0:HALF], wout[:, k, :], states,
                                        start=(k == 0), stop=(k == 1))
                    ins.then_inc(did["o"], 1)
                if name == "h4" and w.valid():
                    pe.wait_ge(left["o"], w.count(2, 2))
                    transposes(s, w, "h4", lambda m: os_[:, m * P:(m + 1) * P])
                if name == "z5" and w.valid():
                    pe.wait_ge(z5_done, w.count(1, 1))
                    transposes(s, w, "z5", lambda m: zh[w.par][:, m, 0:P])
                if name == "logits" and w.valid():
                    pe.wait_ge(left["z5"], w.count(2, 2))
                    dst = claim(s, name, 0)
                    for m in range(TILES):
                        ins = pe.matmul(dst[:, m * NE:(m + 1) * NE],
                                        z5f[:, m * P:(m + 1) * P], wgate[:],
                                        start=True, stop=True)
                    ins.then_inc(did[name], 1)
                if name == "prefix" and w.valid():
                    pe.wait_ge(v["logits"], w.count(1, 1))
                    dst = claim(s, name, 0)
                    wide = TILES * NE
                    pe.matmul(dst[:, 0:wide], tri[:], onehotb[:], start=True, stop=False,
                              skip_group_check=True)
                    for back in range(1, TILES):
                        pe.matmul(dst[:, back * NE:wide], ones[:], onehotb[:, 0:wide - back * NE],
                                  start=False, stop=False, skip_group_check=True)
                    for m in range(TILES):
                        ins = pe.matmul(dst[:, wide:wide + NE], ones[:],
                                        onehotb[:, m * NE:(m + 1) * NE],
                                        start=False, stop=(m == TILES - 1), skip_group_check=True)
                    ins.then_inc(did[name], 1)

            def inputs_of_group(r, g):
                if not r.valid():
                    return
                steps = steps_of(g)
                n = len(steps)
                if g == 0:
                    pe.wait_ge(left["z3"], r.count(2, 2))
                if not r.first() or g >= 2:
                    pe.wait_ge(kept, r.count(4, g - 1))
                inputs = z3f[:].rearrange("p (b j) -> p j b", j=SIDE)[:, steps[0]:steps[-1] + 1:2, :]
                at = rbank[g % 2][:].rearrange("p (j m b) -> p j m b", m=2, b=B)
                for m in range(2):
                    pe.matmul(at[:, 0:n, m, :], wih[:, m, :], inputs,
                              start=(m == 0), stop=False, skip_group_check=True)
                for m in range(2):
                    ins = pe.matmul(at[:, 0:n, m, :], bparts[:, m * P:(m + 1) * P],
                                    ones3[:, 0:n * B].rearrange("p (j b) -> p j b", b=B),
                                    start=False, stop=True, skip_group_check=True)
                ins.then_inc(xp_done, 1)

            def step(s, j):
                if s.first() and j == 0:
                    return
                base = (j % (2 * GROUP)) // 2 * 2 * B
                for part in range(3):
                    pe.wait_ge(part_done[part], s.count(SIDE, j))
                    for m in range(2):
                        for k in range(2):
                            for other in range(3 - part):
                                ins = pe.matmul(
                                    rbank[j % 2][:, base + m * B:base + (m + 1) * B],
                                    whhp[other][:, k, m, :],
                                    hparts[(j + 1) % 2][:, part, k, :],
                                    start=False, stop=True, skip_group_check=True)
                ins.then_inc(stepped, 1)

            all_slots(pe, piece, step)

            def turn(t, i, z, mid, y):
                if z is not None:
                    n = (i + 1) % NBUF
                    pe.wait_ge(tile_in[n], z)
                    if mid is not None and not mid:
                        pe.wait_ge(t_zt, t)
                    for m in range(MT):
                        ins = pe.transpose(bank[n % 2][:, m * P:(m + 1) * P],
                                           rows[n][:, m, 0:P], eye[:])
                    ins.then_inc(t_z, 1)
                if mid is not None:
                    pe.wait_ge(t_zt, t + 1)
                    if not mid:
                        pe.wait_ge(t_hid, t)
                        pe.wait_ge(t_hid1, t)
                    for m in range(2):
                        pe.matmul(pbank[m][:, 0:TS], wexp[i][:, m * P:(m + 1) * P], zt[i % 2][:],
                                  start=True, stop=True).then_inc(t_h, 1)
                if y:
                    k = (i + 1) % 2
                    pe.wait_ge(t_yt, t)
                    if y != "first":
                        pe.wait_ge(t_fin, t - 2)
                    for m in range(MT):
                        ins = pe.transpose(rbank[k][:, m * P:(m + 1) * P],
                                           yt[k][:, m * P:(m + 1) * P], eye[:])
                    ins.then_inc(t_o, 1)
                if mid is not None:
                    for m in range(2):
                        pe.wait_ge((t_hid, t_hid1)[m], t + 1)
                        ins = pe.matmul(bank[2 + i % 2][:, 0:TS],
                                        wexp[i][:, (2 + m) * P:(3 + m) * P], hid[i % 2][:, m, :],
                                        start=(m == 0), stop=(m == 1))
                    ins.then_inc(t_y, 1)

            turn(-1, NBUF - 1, 32, None, None)
            for t in range(NBUF):
                turn(t, t, 32 * ((t + 1) // NBUF + 1), t == 0, (None, "first", "y")[min(t, 2)])
            with pe.Fori(NBUF, NTILES - 2 * NBUF + 1, NBUF) as t:
                for i in range(NBUF):
                    turn(t + i, i, t * (32 // NBUF) + 32 * ((i + 1) // NBUF + 1), False, "y")
            for t in range(NTILES - NBUF, NTILES):
                turn(t, t % NBUF, 32 * ((t + 1) // NBUF + 1) if t + 1 < NTILES else None,
                     False, "y")
            turn(NTILES, 0, None, None, "y")

        @block.scalar
        def _(act):
            act.wait_ge(weights_in, 16 * 12)
            act.wait_ge(zeroed, 1)

            def leave(r, name, job, dst, src, func=ACT.Identity, **kw):
                act.wait_ge(did[name], r.count(PER_ROW[name], job + 1))
                nc.scalar.activation(dst, src, func, **kw).then_inc(left[name], 1)

            def turn_bank(name, job):
                return bank[bank_of(name, job)]

            def leave_transposes(r, name, dst):
                for c, (a, b) in enumerate(SPANS):
                    leave(r, name, c, dst(a, b), turn_bank(name, c)[:, 0:(b - a) * P])

            def normalise(dst, src, key):
                for m in range(TILES):
                    ins = nc.scalar.activation(dst[:, m, 0:P], src[:, m, :], ACT.Identity,
                                               bias=shift[key][:, m:m + 1],
                                               scale=scale[key][:, m:m + 1])
                return ins

            def piece(s, name):
                u, w, v_, d = s.shift(1), s.shift(-1), s.shift(4), s.shift(2)
                if name.startswith("project") and name[8] == "c" and v_.valid():
                    c, name = int(name[7]), name[:8]
                    src = pbank[c]
                    act.wait_ge(did[name], v_.count(1, 1))
                    if c == 0 and not v_.early():
                        act.wait_ge(tok_done, v_.count(1, -1))
                        act.wait_ge(shifts_in[(v_.par + 1) % 2], v_.shift(-1).pair_count(64) - 48)
                        act.wait_ge(did["d"], v_.count(2, -2))
                    nc.scalar.activation(tok[v_.par][0:64, c * HALF:(c + 1) * HALF],
                                         src[0:64, 0:HALF], ACT.Identity, bias=vec[0:64, 0:1])
                    dst = yp[v_.par][64:128, 1:].rearrange("p (b j) -> p b j", j=SIDE + 1)[
                        :, c * B // 2:(c + 1) * B // 2, 0:SIDE]
                    nc.scalar.activation(dst, src[64:128, 0:HALF].rearrange(
                        "p (b j) -> p b j", j=SIDE), ACT.Identity).then_inc(left[name], 1)
                if name == "d" and d.valid():
                    leave_transposes(d, "d", lambda a, b: tokT[:, a:b, :])
                if name == "e" and u.valid():
                    leave_transposes(u, "e", lambda a, b: z1f[:, a * P:b * P])
                if name in ("gates0", "gates1") and u.valid():
                    c = int(name[5])
                    leave(u, "sigmoid", c, gate[:, c * HALF:(c + 1) * HALF],
                          turn_bank("sigmoid", c)[:, 0:HALF], ACT.Sigmoid)
                if name in ("y0", "y1") and u.valid():
                    c = int(name[1])
                    leave(u, "y", c, ys[:, c * HALF:(c + 1) * HALF],
                          turn_bank("y", c)[:, 0:HALF], bias=byscaled[:, 0:1], scale=HSCALE)
                if name in ("open0", "open1") and u.valid():
                    c = int(name[4])
                    cols = slice(c * HALF, (c + 1) * HALF)
                    act.wait_ge(clipped, u.count(2, c + 1))
                    nc.scalar.activation(decay[:, cols], gate[:, cols], ACT.Identity, bias=1.0,
                                         scale=a_minus_1[:, 0:1]).then_inc(decayed, 1)
                if name.startswith("keep") and s.valid():
                    g = int(name[4])
                    steps = steps_of(g)
                    act.wait_ge(rest_done, s.count(SIDE, steps[-1] + 1))
                    if g == 0 and not s.early():
                        act.wait_ge(did["o"], s.count(2, -2))
                    nc.scalar.activation(
                        hr[s.par][:, steps[0]:steps[-1] + 1:2, :, :],
                        rbank[g % 2][:, 0:len(steps) * 2 * B].rearrange(
                            "p (j m b) -> p j m b", m=2, b=B), ACT.Relu).then_inc(kept, 1)
                if name == "n1" and d.valid():
                    act.wait_ge(scaled["tok"], d.count(1, 1))
                    normalise(h1[d.par], tokT, "tok").then_inc(n1_done, 1)
                if name == "z1n" and d.valid():
                    act.wait_ge(scaled["h1"], d.count(1, 1))
                    if not d.first():
                        act.wait_ge(did["e"], d.count(2, 0))
                    normalise(z1, h1[d.par], "h1").then_inc(z1_done, 1)
                if name == "z3n" and u.valid():
                    act.wait_ge(scaled["h2"], u.count(1, 1))
                    if not u.first():
                        act.wait_ge(did["z3"], u.count(2, 0))
                    normalise(z3, h2, "h3").then_inc(z3_done, 1)
                if name == "h3n" and s.valid():
                    if not s.early():
                        act.wait_ge(left["h4"], s.count(2, -2))
                    normalise(h3[s.par], h2, "h2").then_inc(h3_done, 1)
                if name == "z5n" and w.valid():
                    act.wait_ge(scaled["h4"], w.count(1, 1))
                    mine = zh[w.par]
                    normalise(mine, mine[:, :, P:2 * P], "h4").then_inc(z5_done, 1)
                if name == "z3" and u.valid():
                    if not u.first():
                        act.wait_ge(xp_done, u.count(4, 0))
                    leave_transposes(u, "z3", lambda a, b: z3f[:, a * P:b * P])
                if name in ("o0", "o1") and w.valid():
                    c = int(name[1])
                    leave(w, "o", c, os_[:, c * HALF:(c + 1) * HALF],
                          turn_bank("o", c)[:, 0:HALF], bias=wv(V_BO))
                if name == "z5" and w.valid():
                    leave_transposes(w, "z5", lambda a, b: z5f[:, a * P:b * P])
            all_slots(act, piece, lambda s, j: None)
            write_pads(act, range(1, NE, 2))

            def tile_z(t, n, first):
                act.wait_ge(t_z, t + 1)
                if not first:
                    act.wait_ge(t_h, 2 * (t - 1))
                nc.scalar.activation(zt[n % 2][:], bank[n % 2][:, 0:TS], ACT.Identity)\
                    .then_inc(t_zt, 1)

            def tile_rest(t, i, first):
                act.wait_ge(t_h, 2 * t + 1)
                if not first:
                    act.wait_ge(t_y, t - 1)
                nc.scalar.activation(hid[i % 2][:, 0, :], pbank[0][:, 0:TS], ACT.Relu,
                                     bias=wexp[i][:, 4 * P:4 * P + 1]).then_inc(t_hid, 1)
                act.wait_ge(t_y, t + 1)
                if not first:
                    act.wait_ge(t_o, t - 1)
                nc.scalar.activation(yt[i % 2][:], bank[2 + i % 2][:, 0:TS], ACT.Identity,
                                     bias=wexp[i][:, 4 * P + 2:4 * P + 3]).then_inc(t_yt, 1)

            tile_z(0, 0, True)
            for t in range(NBUF):
                tile_z(t + 1, t + 1, t + 1 < 2)
                tile_rest(t, t, t < 2)
            with act.Fori(NBUF, NTILES - 2 * NBUF + 1, NBUF) as t:
                for i in range(NBUF):
                    tile_z(t + i + 1, i + 1, False)
                    tile_rest(t + i, i, False)
            for t in range(NTILES - NBUF, NTILES):
                if t + 1 < NTILES:
                    tile_z(t + 1, t + 1, False)
                tile_rest(t, t % NBUF, False)

        @block.gpsimd
        def _(pool):
            links = [0]

            def link(ins, s):
                links[0] += 1
                ins.then_inc(pool_chain, 1)
                if isinstance(s.base, int):
                    pool.wait_ge(pool_chain, links[0])
                else:
                    pool.wait_ge(pool_chain, (s.base - LOOP[0]) * POOL_LINKS + links[0])

            links_before = [0]

            def steady():
                turns = (LOOP[1] - LOOP[0]) // 2
                assert links[0] - links_before[0] == 2 * POOL_LINKS, links[0] - links_before[0]
                links[0] += (turns - 1) * 2 * POOL_LINKS

            pool.wait_ge(weights_in, 16 * 12)
            pool.wait_ge(consts_done, 1)

            def carry(cell=0, count=carried):
                nc.gpsimd.tensor_tensor(carrier[:, cell:cell + 1], carrier[:, 2:3],
                                        carrier[:, 2:3], ALU.add).then_inc(count, 1)

            def small(dst, a, b, op):
                return nc.gpsimd.tensor_tensor(dst[:], a[:], b[:], op)

            def scale_and_shift(s, r, key):
                pool.wait_ge(moments_done[key], r.count(1, 1))
                link(small(scale[key], veps[key], minus_half, ALU.pow), s)
                small(shift[key], minus_mean[key], scale[key], ALU.mult).then_inc(scaled[key], 1)

            def piece(s, name):
                u, w, d = s.shift(1), s.shift(-1), s.shift(2)
                if name == "tok_stats" and d.valid():
                    scale_and_shift(s, d, "tok")
                if name == "n1" and d.valid():
                    g = gb[:, 0, :].unsqueeze(1).broadcast_to([P, TILES, P])
                    b = gb[:, 1, :].unsqueeze(1).broadcast_to([P, TILES, P])
                    pool.wait_ge(n1_done, d.count(1, 1))
                    mine = h1[d.par][:]
                    nc.gpsimd.tensor_tensor(mine, mine, g, ALU.mult).then_inc(affine, 1)
                    pool.wait_ge(affine, d.count(2, 1))
                    nc.gpsimd.tensor_tensor(mine, mine, b, ALU.add).then_inc(affine, 1)
                if name == "h1_stats" and d.valid():
                    scale_and_shift(s, d, "h1")
                if name == "h2_stats" and u.valid():
                    pool.wait_ge(moments_done["h2"], u.count(1, 1))
                    link(small(rstd["h2"], veps["h2"], minus_half, ALU.pow), s)
                    link(small(scale["h2"], rstd["h2"], one7, ALU.add), s)
                    link(small(veps["h3"], scale["h2"], scale["h2"], ALU.mult), s)
                    link(nc.gpsimd.tensor_tensor(veps["h3"][:], veps["h3"][:], mv["h2"][:, :, 1],
                                                 ALU.mult), s)
                    link(small(veps["h3"], veps["h3"], eps7, ALU.add), s)
                    link(small(rstd["h3"], veps["h3"], minus_half, ALU.pow), s)
                    link(small(scale["h3"], scale["h2"], rstd["h3"], ALU.mult), s)
                    small(shift["h2"], minus_mean["h2"], rstd["h2"], ALU.mult)
                    small(shift["h3"], minus_mean["h2"], scale["h3"], ALU.mult)\
                        .then_inc(scaled["h2"], 1)
                if name == "h4_stats" and w.valid():
                    scale_and_shift(s, w, "h4")
                if name == "place" and w.valid():
                    pool.wait_ge(v["place"], w.count(1, 1))
                    carry()
                    for m in range(TILES):
                        nc.gpsimd.indirect_dma_start(
                            places, bass.IndirectOffsetOnAxis(ap=placeu[w.par][:, m:m + 1], axis=0),
                            zh[w.par][:, m, :], None, bounds_check=NE * CAP - 1,
                            oob_is_err=False).then_inc(scattered[w.par], 16)

            all_slots(pool, piece, lambda s, j: None,
                      lambda: links_before.append(links_before.pop() + links[0]), steady)

            def tile_out(t, i):
                pool.wait_ge(t_fin, t + 1)
                if not isinstance(t, int) or t:
                    pool.wait_ge(t_carried, t)
                carry(1, t_carried)
                for m in range(MT):
                    nc.gpsimd.indirect_dma_start(
                        out, bass.IndirectOffsetOnAxis(ap=fid[i % NFIN][:, m:m + 1], axis=0),
                        fin[i % NFIN][:, m, :], None, bounds_check=TOKENS - 1,
                        oob_is_err=False).then_inc(out_done[i % NFIN], 16)

            for t in range(NBUF):
                tile_out(t, t)
            with pool.Fori(NBUF, NTILES - NBUF + 1, NBUF) as t:
                for i in range(NBUF):
                    tile_out(t + i, i)
            for i in range(NFIN):
                pool.wait_ge(out_done[i], 16 * MT * NTILES // NFIN)

        @block.vector
        def _(dve):
            links = [0]

            def link(ins, s=Row(0, 0)):
                links[0] += 1
                ins.then_inc(dve_chain, 1)
                if isinstance(s.base, int):
                    dve.wait_ge(dve_chain, links[0])
                else:
                    dve.wait_ge(dve_chain, (s.base - LOOP[0]) * LINKS + links[0])

            link(dve.memset(zeros[:], 0.0))
            for i in range(2):
                link(dve.memset(yp[i][:], 0.0))
            dve.sem_inc(zeroed, 1)
            link(dve.memset(one7[:], 1.0))
            link(dve.memset(eps7[:], EPS))
            link(dve.memset(minus_half[:], -0.5))
            link(dve.memset(ones[:], 1.0))
            link(dve.memset(carrier[:], 0.0))
            link(dve.memset(ones3[:], 1.0))
            link(dve.memset(row8["one"][:], 1.0))
            link(dve.memset(pad[:], 0.0))
            link(dve.memset(pad[:, :, 2 * P:2 * P + 1], NOWHERE))
            for i in range(2):
                link(dve.memset(zh[i][:, :, 2 * P:WIDE], 0.0))
            for e in range(NE):
                link(dve.memset(rank[:, e:e + 1], float(NE - e)))
                link(dve.memset(region[:, e:e + 1], float(e * CAP)))
            for t in range(NTILES):
                ins = dve.memset(tilex[:, t, :], float(t))
            link(ins)
            link(dve.tensor_copy(free[:], region[:]))
            dve.wait_ge(weights_in, 16 * 12)
            link(dve.tensor_tensor(brow[:, 0, :], brow[:, 0, :], brow[:, 1, :], ALU.add))
            for i in range(3):
                link(dve.tensor_copy(bsplit[:, i, :], brow[:, 0, :]))
                link(dve.tensor_tensor(brow[:, 0, :], brow[:, 0, :], bsplit[:, i, :],
                                       ALU.subtract))
                link(dve.tensor_copy(whhp[i][:], whh[:]))
                link(dve.tensor_tensor(whh[:], whh[:], whhp[i][:], ALU.subtract))
            dve.sem_inc(split_done, 1)
            link(dve.tensor_copy(tri[:], tri32[:]))
            link(dve.tensor_scalar(byscaled[:], wv(V_BY), HSCALE, None, ALU.mult))
            link(dve.tensor_scalar(a_minus_1[:], wv(V_A), -1.0, None, ALU.add))
            dve.sem_inc(consts_done, 1)

            def turn_bank(name, job):
                return bank[bank_of(name, job)]

            links_before = [0]

            def steady():
                turns = (LOOP[1] - LOOP[0]) // 2
                assert links[0] - links_before[0] == 2 * LINKS, links[0] - links_before[0]
                links[0] += (turns - 1) * 2 * LINKS

            def moments(s, key, src):
                for m in range(TILES):
                    ins = dve.bn_stats(stats[key][:, m, :], src[:, m, :])
                link(ins, s)
                dve.memset(scratch[:], 0.0).then_inc(scratched, 1)
                for m in range(TILES):
                    ins = dve.bn_aggr(mv[key][:, m, :], stats[key][:, m, :])
                link(ins, s)
                dve.tensor_scalar(minus_mean[key][:], mv[key][:, :, 0], -1.0, None, ALU.mult)
                dve.tensor_scalar(veps[key][:], mv[key][:, :, 1], EPS, None, ALU.add)\
                    .then_inc(moments_done[key], 1)

            def piece(s, name):
                u, w, f, d = s.shift(1), s.shift(-1), s.shift(3), s.shift(2)
                if name == "finish_tok" and f.valid():
                    dve.wait_ge(shifts_in[f.par], f.pair_count(64))
                    dve.wait_ge(left["project1"], f.count(1, 1))
                    if not f.early():
                        dve.wait_ge(did["d"], f.count(2, -2))
                    own = yp[f.par][64:128, 1:].rearrange("p (b j) -> p b j", j=SIDE + 1)
                    other = sh[f.par][64:128, :].rearrange("p (b j) -> p b j", j=SIDE + 1)
                    dve.scalar_tensor_tensor(
                        tok[f.par][64:128, :].rearrange("p (b j) -> p b j", j=SIDE),
                        own[:, :, 0:SIDE], vec[64:128, 0:1], other[:, :, 0:SIDE],
                        ALU.add, ALU.add).then_inc(tok_done, 1)
                if name == "tok_stats" and d.valid():
                    dve.wait_ge(left["d"], d.count(2, 2))
                    moments(s, "tok", tokT)
                if name == "h1_stats" and d.valid():
                    dve.wait_ge(affine, d.count(2, 2))
                    moments(s, "h1", h1[d.par])
                if name in ("open0", "open1") and u.valid():
                    c = int(name[4])
                    cols = slice(c * HALF, (c + 1) * HALF)
                    dve.wait_ge(left["sigmoid"], u.count(2, c + 1))
                    dve.tensor_scalar(gate[:, cols], gate[:, cols], 0.05, 0.95, ALU.max, ALU.min)\
                        .then_inc(clipped, 1)
                    dve.wait_ge(clipped, u.count(2, c + 1))
                    dve.wait_ge(did["inputs"], u.count(2, c + 1))
                    dve.scalar_tensor_tensor(inp[:, cols], turn_bank("inputs", c)[:, 0:HALF],
                                             wv(V_BH), gate[:, cols], ALU.add, ALU.mult)\
                        .then_inc(left["inputs"], 1)
                if name == "scan" and u.valid():
                    dve.wait_ge(left["inputs"], u.count(2, 2))
                    dve.wait_ge(decayed, u.count(2, 2))
                    a3 = decay[:].rearrange("p (b j) -> p b j", j=SIDE)
                    b3 = inp[:].rearrange("p (b j) -> p b j", j=SIDE)
                    if not u.first():
                        before = hs[1 - u.par][:].rearrange("p (b j) -> p b j", j=SIDE)
                        link(dve.tensor_tensor(first_term[:], a3[:, :, 0], before[:, :, SIDE - 1],
                                               ALU.mult), s)
                        link(dve.tensor_tensor(b3[:, :, 0], b3[:, :, 0], first_term[:], ALU.add), s)
                    link(dve.memset(a3[:, :, 0], 0.0), s)
                    if not u.early():
                        dve.wait_ge(did["y"], u.count(2, -2))
                    dve.tensor_tensor_scan(hs[u.par][:], decay[:], inp[:], 0.0, ALU.mult, ALU.add)\
                        .then_inc(scan_done, 1)
                    dve.wait_ge(scan_done, u.count(1, 1))
                if name == "h2_add" and u.valid():
                    if not u.first():
                        dve.wait_ge(h3_done, u.count(1, 0))
                    for c, (a, b) in enumerate(SPANS):
                        dve.wait_ge(did["h2"], u.count(2, c + 1))
                        dve.tensor_tensor(h2[:, a:b, :], h1[u.par][:, a:b, :],
                                          turn_bank("h2", c)[:, 0:(b - a) * P].rearrange(
                                              "p (m f) -> p m f", f=P), ALU.add)\
                            .then_inc(left["h2"], 1)
                if name == "h2_stats" and u.valid():
                    dve.wait_ge(left["h2"], u.count(2, 2))
                    moments(s, "h2", h2)
                if name == "h4_add" and w.valid():
                    mine = zh[w.par]
                    if not w.early():
                        dve.wait_ge(scattered[w.par], w.pair_count(16 * TILES) - 16 * TILES)
                    dve.wait_ge(h3_done, w.count(1, 1))
                    for c, (a, b) in enumerate(SPANS):
                        dve.wait_ge(did["h4"], w.count(2, c + 1))
                        dve.tensor_tensor(mine[:, a:b, P:2 * P], h3[w.par][:, a:b, :],
                                          turn_bank("h4", c)[:, 0:(b - a) * P].rearrange(
                                              "p (m f) -> p m f", f=P), ALU.add)\
                            .then_inc(left["h4"], 1)
                    link(dve.tensor_copy(mine[:, :, 2 * P], ids[:]), s)
                    link(dve.tensor_scalar(ids[:], ids[:], float(ROW), None, ALU.add), s)
                if name == "h4_stats" and w.valid():
                    dve.wait_ge(left["h4"], w.count(2, 2))
                    moments(s, "h4", zh[w.par][:, :, P:2 * P])
                if name == "pick" and w.valid():
                    dve.wait_ge(did["logits"], w.count(1, 1))
                    lg_in = turn_bank("logits", 0)[:, 0:TILES * NE].rearrange(
                        "p (m e) -> p m e", e=NE)
                    dve.tensor_tensor(lg[:], lg_in, bgate[:].unsqueeze(1).broadcast_to(
                        [P, TILES, NE]), ALU.add).then_inc(left["logits"], 1)
                    dve.wait_ge(left["logits"], w.count(1, 1))
                    link(dve.tensor_reduce(lmax[:], lg[:], AX.X, ALU.max), s)
                    link(dve.tensor_tensor(lg[:], lg[:], lmax[:].unsqueeze(2).broadcast_to(
                        [P, TILES, NE]), ALU.is_equal), s)
                    link(dve.tensor_tensor(lg[:], lg[:], rank[:].unsqueeze(1).broadcast_to(
                        [P, TILES, NE]), ALU.mult), s)
                    link(dve.tensor_reduce(lmax[:], lg[:], AX.X, ALU.max), s)
                    if not w.first():
                        dve.wait_ge(did["prefix"], w.count(1, 0))
                    link(dve.tensor_tensor(onehot[:], lmax[:].unsqueeze(2).broadcast_to(
                        [P, TILES, NE]), rank[:].unsqueeze(1).broadcast_to([P, TILES, NE]),
                        ALU.is_equal), s)
                    dve.tensor_copy(onehotb[:].rearrange("p (m e) -> p m e", e=NE), onehot[:])\
                        .then_inc(v["logits"], 1)
                if name == "place" and w.valid():
                    dve.wait_ge(did["prefix"], w.count(1, 1))
                    src = turn_bank("prefix", 0)
                    wide = TILES * NE
                    link(dve.tensor_tensor(place[:], src[:, 0:wide].rearrange(
                        "p (m e) -> p m e", e=NE), free[:].unsqueeze(1).broadcast_to(
                            [P, TILES, NE]), ALU.add), s)
                    dve.tensor_tensor(free[:], free[:], src[:, wide:wide + NE], ALU.add)\
                        .then_inc(left["prefix"], 1)
                    link(dve.tensor_tensor(place[:], place[:], onehot[:], ALU.mult), s)
                    link(dve.tensor_reduce(placef[:], place[:], AX.X, ALU.add), s)
                    if not w.early():
                        dve.wait_ge(scattered[w.par], w.pair_count(16 * TILES) - 16 * TILES)
                    dve.tensor_copy(placeu[w.par][:], placef[:]).then_inc(v["place"], 1)
                    dve.wait_ge(left["prefix"], w.count(1, 1))

            def step(s, j):
                if s.first() and j == 0:
                    dve.wait_ge(xp_done, 1)
                else:
                    dve.wait_ge(stepped, s.count(SIDE, j))
                base = (j % (2 * GROUP)) // 2 * 2 * B
                sums = rbank[j % 2][:, base:base + 2 * B].rearrange(
                    "p (m b) -> p m b", b=B)
                parts = hparts[j % 2]
                dve.tensor_scalar(parts[:, 0, :, :], sums, 0.0, None, ALU.max)\
                    .then_inc(part_done[0], 1)
                dve.wait_ge(part_done[0], s.count(SIDE, j + 1))
                dve.scalar_tensor_tensor(parts[:, 1, :, :], sums, 0.0, parts[:, 0, :, :],
                                         ALU.max, ALU.subtract).then_inc(part_done[1], 1)
                dve.scalar_tensor_tensor(rest[:], sums, 0.0, parts[:, 0, :, :],
                                         ALU.max, ALU.subtract).then_inc(rest_done, 1)
                dve.wait_ge(part_done[1], s.count(SIDE, j + 1))
                dve.wait_ge(rest_done, s.count(SIDE, j + 1))
                dve.tensor_tensor(parts[:, 2, :, :], rest[:], parts[:, 1, :, :], ALU.subtract)\
                    .then_inc(part_done[2], 1)

            all_slots(dve, piece, step, lambda: links_before.append(links_before.pop() + links[0]),
                      steady)

            count, tiles, ends, starts, one = (row8[n][:] for n in (
                "count", "tiles", "ends", "starts", "one"))
            dve.tensor_copy(freeu[:], free[0:1, :]).then_inc(ends_known, 1)
            link(dve.tensor_tensor(count, free[0:1, :], region[0:1, :], ALU.subtract))
            link(dve.tensor_scalar(count, count, float(TS - 1), None, ALU.add))
            link(dve.tensor_copy(row8i[:], count))
            link(dve.tensor_single_scalar(row8i[:], row8i[:], TS.bit_length() - 1,
                                          ALU.logical_shift_right))
            link(dve.tensor_copy(tiles, row8i[:]))
            link(dve.tensor_tensor_scan(ends, one, tiles, 0.0, ALU.mult, ALU.add))
            link(dve.tensor_tensor(starts, ends, tiles, ALU.subtract))
            wide = [1, NTILES, NE]

            def over_tiles(a):
                return a.unsqueeze(1).broadcast_to(wide)

            a, b = tab["a"], tab["b"]
            link(dve.tensor_tensor(a[:], tilex[:], over_tiles(starts), ALU.is_ge))
            link(dve.tensor_tensor(b[:], tilex[:], over_tiles(ends), ALU.is_lt))
            link(dve.tensor_tensor(a[:], a[:], b[:], ALU.mult))
            link(dve.tensor_reduce(tilef["any"][:], a[:], AX.X, ALU.add))
            link(dve.tensor_tensor(b[:], tilex[:], over_tiles(starts), ALU.subtract))
            link(dve.scalar_tensor_tensor(b[:], b[:], float(TS), over_tiles(region[0:1, :]),
                                          ALU.mult, ALU.add))
            link(dve.tensor_tensor(b[:], b[:], a[:], ALU.mult))
            link(dve.tensor_reduce(tilef["place"][:], b[:], AX.X, ALU.add))
            link(dve.tensor_scalar(count, rank[0:1, :], -1.0, float(NE), ALU.mult, ALU.add))
            link(dve.tensor_tensor(b[:], a[:], over_tiles(count), ALU.mult))
            link(dve.tensor_reduce(tilef["expert"][:], b[:], AX.X, ALU.add))
            link(dve.tensor_scalar(tilef["any"][:], tilef["any"][:], -1.0, 1.0,
                                   ALU.mult, ALU.add))
            link(dve.scalar_tensor_tensor(tilef["place"][:], tilef["any"][:],
                                          free[0:1, NE - 1:NE], tilef["place"][:],
                                          ALU.mult, ALU.add))
            link(dve.tensor_copy(tileu["place"][:], tilef["place"][:]))
            dve.tensor_copy(tileu["expert"][:], tilef["expert"][:]).then_inc(tables_done, 1)

            def tile_hidden(t, i, first):
                dve.wait_ge(t_h, 2 * t + 2)
                if not first:
                    dve.wait_ge(t_y, t - 1)
                dve.tensor_scalar(hid[i % 2][:, 1, :], pbank[1][:, 0:TS],
                                  wexp[i][:, 4 * P + 1:4 * P + 2], 0.0, ALU.add, ALU.max)\
                    .then_inc(t_hid1, 1)

            def tile_fin(t, i, first):
                n = i % NFIN
                if first:
                    dve.wait_ge(t_o, t + 1)
                else:
                    dve.wait_ge(out_done[n], first_use(t, n))
                    dve.wait_ge(t_o, t + 1)
                dve.tensor_copy(fid[n][:], rows[i][:, :, 2 * P]).then_inc(t_ids, 1)
                dve.wait_ge(t_ids, t + 1)
                dve.tensor_tensor(fin[n][:], rows[i][:, :, P:2 * P],
                                  rbank[i % 2][:, 0:TS].rearrange("p (m f) -> p m f", f=P),
                                  ALU.add).then_inc(t_fin, 1)

            def first_use(t, n):
                return (t - n) * (16 * MT // NFIN)

            for t in range(NBUF):
                tile_hidden(t, t, t < 2)
                if t:
                    tile_fin(t - 1, t - 1, t <= NFIN)
            with dve.Fori(NBUF, NTILES - NBUF + 1, NBUF) as t:
                for i in range(NBUF):
                    tile_hidden(t + i, i, False)
                    tile_fin(t + i - 1, (i - 1) % NBUF, False)
            tile_fin(NTILES - 1, NBUF - 1, False)


def patch_rows(x):
    t = np.asarray(x).reshape(B, 3, SIDE, PATCH, SIDE, PATCH).transpose(2, 1, 3, 5, 0, 4)
    return np.ascontiguousarray(t.reshape(SIDE, KC, P, ROW).transpose(0, 2, 1, 3))


def patch_weights(w_main, w_sx, w_sy):
    d, ds, h = w_main.shape[0], w_sx.shape[0], PATCH // 2
    w = np.zeros((d + 4 * ds, 3, PATCH, PATCH), w_main.dtype)
    w[:d] = w_main.reshape(d, 3, PATCH, PATCH)
    sx, sy = (a.reshape(ds, 3, PATCH, PATCH) for a in (w_sx, w_sy))
    w[d:d + ds, :, :, h:] = sx[:, :, :, :h]
    w[d + ds:d + 2 * ds, :, :, :h] = sx[:, :, :, h:]
    w[d + 2 * ds:d + 3 * ds, :, h:, :] = sy[:, :, :h, :]
    w[d + 3 * ds:, :, :h, :] = sy[:, :, h:, :]
    return np.ascontiguousarray(w.reshape(-1, KC, P).transpose(2, 1, 0))


def kernel(**inputs):
    import concourse.bacc as bacc
    from concourse.bass_utils import run_bass_kernel_spmd

    a = {k: np.asarray(t) for k, t in inputs.items()}
    f = a["x"].dtype
    tok, at, rn, ff = "L0_tok_", "L0_attn_", "L1_attn_", "L1_ffn_"
    columns = [np.concatenate([a[tok + "b_main"], a[tok + "b_sx"], a[tok + "b_sx"],
                               a[tok + "b_sy"], a[tok + "b_sy"]]),
               a[at + "A"], a[at + "bias_h"], a[at + "bias_y"],
               a[rn + "b_out"]]
    w1 = a[ff + "W1"]
    w2 = a[ff + "W2"].reshape(NE, 2, P, P).transpose(0, 2, 1, 3).reshape(NE, P, 2 * P)
    b1 = a[ff + "b1"].reshape(NE, 2, P).transpose(0, 2, 1)
    b2 = a[ff + "b2"][:, :, None]
    arrays = {
        "x": patch_rows(a["x"]),
        "w_tok": patch_weights(a[tok + "W_main"], a[tok + "W_sx"], a[tok + "W_sy"]),
        "w_attn": np.stack([a[at + n].T for n in ("Wg", "B", "C", "D")], 1),
        "vectors": np.stack(columns, 1),
        "rows_gb": np.broadcast_to(np.stack([a[tok + "ln_g"], a[tok + "ln_b"]]), (P, 2, P)),
        "w_ih": a[rn + "W_ih"].reshape(2, P, P).transpose(2, 0, 1),
        "w_hh": a[rn + "W_hh"].reshape(2, P, 2, P).transpose(3, 2, 0, 1),
        "w_out": a[rn + "W_out"].reshape(P, 2, P).transpose(2, 1, 0),
        "b_rnn": np.stack([a[rn + "b_ih"], a[rn + "b_hh"]])[None],
        "w_gate": a[ff + "Wg"],
        "b_gate": np.broadcast_to(a[ff + "bg"], (P, NE)),
        "ident": np.eye(P, dtype=f),
        "first_ids": np.arange(ROW, dtype=f).reshape(TILES, P).T,
        "triangle": np.triu(np.ones((P, P), f), 1),
        "experts": np.concatenate([w1, w2, b1, b2, np.zeros_like(b2)], 2),
    }
    arrays = {k: np.ascontiguousarray(t) for k, t in arrays.items()}
    nc = bacc.Bacc("TRN2", target_bir_lowering=False, num_devices=1)
    args = [nc.dram_tensor(f"in_{k}", t.shape, mybir.dt.from_np(t.dtype),
                           kind="ExternalInput").ap() for k, t in arrays.items()]
    places = nc.dram_tensor("places", (NE * CAP, WIDE), F32, kind="Internal").ap()
    out = nc.dram_tensor("out", (TOKENS, P), F32, kind="ExternalOutput").ap()
    build(nc, *args, places, out)
    r = run_bass_kernel_spmd(nc, [{f"in_{k}": t for k, t in arrays.items()}], core_ids=[0])
    got = np.asarray(r.results[0]["out"])
    got = got.reshape(SIDE, B, SIDE, P).transpose(1, 0, 2, 3)
    return np.ascontiguousarray(got.reshape(B, SIDE * SIDE, P))
```

```python
from contextlib import ExitStack

import concourse.bass as bass
import numpy as np
from concourse import mybir

F32 = mybir.dt.float32
BF16 = mybir.dt.bfloat16
U32 = mybir.dt.uint32
I32 = mybir.dt.int32
ALU = mybir.AluOpType
ACT = mybir.ActivationFunctionType
AX = mybir.AxisListType

P = 128
B, SIDE, PATCH = 64, 14, 16
ROW = B * SIDE
HALF = ROW // 2
TILES = ROW // P
KC = 3 * PATCH * PATCH // P
PADDED = B * (SIDE + 1)
GROUP = 4
NE = 8
TOKENS = SIDE * ROW
TS = 256
MT = TS // P
PLACE_BITS = (TOKENS + TS - 1).bit_length()
CAP = 1 << PLACE_BITS
NTILES = (TOKENS + NE * (TS - 1)) // TS
WIDE = 2 * P + 4
WEXP = 4 * P + 4
NBUF = 8
NFIN = 8
NOWHERE = 60000.0
EPS = 1e-5
HSCALE = float(P) ** -0.5
SPANS = {"h2": ((0, 3), (3, TILES)), "h4": ((0, 3), (3, TILES)),
         "e": ((0, 4), (4, TILES)), "d": ((0, 4), (4, TILES)), "z3": ((0, 4), (4, TILES)),
         "z5": ((0, 4), (4, TILES))}
V_TOKB, V_A, V_BH, V_BY, V_BO, NVEC = range(6)

LOOP = (2, 8)
LINKS = 16
POOL_LINKS = 10
PLAN = [
    ["finish_tok", "e", "xp1"],
    ["d", "tok_stats", "tok_mv", "gates0"],
    ["o0", "gates1", "open0"],
    ["o1", "open1", "n1"],
    ["h3n", "scan", "project0a", "h4"],
    ["y0", "h4_add", "h4_stats", "y1"],
    ["h1_stats", "h1_mv", "project0b", "keep0"],
    ["h2_add", "h4_mv", "h2", "keep1", "z1n", "h2_stats", "xp2", "project0c", "project1a"],
    ["h2_mv", "xp3", "z5n"],
    ["project1b", "project1c"],
    ["z5"],
    ["z3n"],
    ["keep2", "logits", "z3", "pick"],
    ["prefix", "keep3", "place", "xp0"],
]
JOBS = {"e": (("e", 0), ("e", 1), 1), "gates0": (("sigmoid", 0), ("inputs", 0), 1),
        "gates1": (("sigmoid", 1), ("inputs", 1), 1), "o0": (("o", 0), -1), "o1": (("o", 1), -1),
        "h4": (("h4", 0), ("h4", 1), -1), "y0": (("y", 0), 1), "y1": (("y", 1), 1),
        "h2": (("h2", 0), ("h2", 1), 1), "d": (("d", 0), ("d", 1), 2),
        "z5": (("z5", 0), ("z5", 1), -1), "logits": (("logits", 0), -1),
        "z3": (("z3", 0), ("z3", 1), 1), "prefix": (("prefix", 0), -1)}
PER_ROW = {"e": 2, "sigmoid": 2, "inputs": 2, "o": 2, "h4": 2, "y": 2, "h2": 2, "d": 2, "z5": 2,
           "logits": 1, "z3": 2, "prefix": 1, "project0": 1, "project1": 1}
GENERAL = 4


class Row:

    def __init__(self, base, off):
        self.base, self.off, self.par = base, off, off % 2

    def valid(self):
        return not isinstance(self.base, int) or 0 <= self.base + self.off < SIDE

    def shift(self, by):
        return Row(self.base, self.off + by)

    def first(self):
        return isinstance(self.base, int) and self.base + self.off == 0

    def early(self):
        return isinstance(self.base, int) and self.base + self.off < 2

    def index(self):
        return self.base + self.off

    def count(self, per_row, n):
        return self.base * per_row + (self.off * per_row + n)

    def pair_count(self, per_row):
        if isinstance(self.base, int):
            return per_row * ((self.base + self.off) // 2 + 1)
        return self.base * (per_row // 2) + per_row * (self.off // 2 + 1)


def stepless_order():
    late = ("h1_stats", "h1_mv")
    order = [name for group in PLAN for name in group if name not in late + ("z1n",)]
    at = order.index("h2_mv") + 1
    return order[:at] + list(late) + order[at:] + ["z1n"]


def bank_turns():
    turns = []
    for name in (name for group in PLAN for name in group if name in JOBS):
        *jobs, off = JOBS[name]
        turns += [(kind, number, off) for kind, number in jobs]
    return turns


def bank_of(kind, job):
    return [t[:2] for t in TURNS].index((kind, job)) % GENERAL


TURNS = bank_turns()


def steps_of(group):
    first = group // 2 * 2 * GROUP
    return range(first + group % 2, min(SIDE, first + 2 * GROUP), 2)


def build(nc, x, w_tok, w_attn, vectors, rows_gb, w_ih, w_hh, w_out, b_rnn, w_gate, b_gate,
          ident, first_ids, triangle, experts, places, out):
    with ExitStack() as ctx:
        def sb(name, shape, dt=F32):
            return ctx.enter_context(nc.sbuf_tensor(name, shape, dt))

        def psum(name):
            return ctx.enter_context(nc.psum_tensor(name, [P, 512], F32))

        def sem(name):
            return ctx.enter_context(nc.semaphore(name))

        wtok = sb("wtok", [P, KC, P])
        wattn = sb("wattn", [P, 4, P])
        vec = sb("vec", [P, NVEC])
        byscaled = sb("byscaled", [P, 1])
        a_minus_1 = sb("a_minus_1", [P, 1])
        brow = sb("brow", [1, 2, 2 * P])
        bsplit = sb("bsplit", [1, 3, 2 * P], BF16)
        bparts = sb("bparts", [3, 2 * P], BF16)
        ones3 = sb("ones3", [3, GROUP * B], BF16)
        gb = sb("gb", [P, 2, P])
        wih = sb("wih", [P, 2, P])
        whh = sb("whh", [P, 2, 2, P])
        whhp = [sb(f"whhp{i}", [P, 2, 2, P], BF16) for i in range(3)]
        wout = sb("wout", [P, 2, P])
        wgate = sb("wgate", [P, NE])
        bgate = sb("bgate", [P, NE])
        eye = sb("eye", [P, P])
        tri32 = sb("tri32", [P, P])
        tri = sb("tri", [P, P], BF16)
        ones = sb("ones", [P, P], BF16)
        region = sb("region", [P, NE])
        free = sb("free", [P, NE])
        ids = sb("ids", [P, TILES])
        rank = sb("rank", [P, NE])
        minus_half = sb("minus_half", [P, TILES])
        zeros = sb("zeros", [P, PADDED])
        xs = [sb(f"xs{i}", [P, KC, ROW]) for i in range(2)]
        yp = [sb(f"yp{i}", [P, 1 + PADDED]) for i in range(2)]
        sh = [sb(f"sh{i}", [P, PADDED]) for i in range(2)]
        tok = [sb(f"tok{i}", [P, ROW]) for i in range(2)]
        tokT = sb("tokT", [P, TILES, P])
        h1 = [sb(f"h1_{i}", [P, TILES, P]) for i in range(2)]
        z1 = sb("z1", [P, TILES, P])
        z1f = sb("z1f", [P, ROW])
        gate = sb("gate", [P, ROW])
        inp = sb("inp", [P, ROW])
        decay = sb("decay", [P, ROW])
        first_term = sb("first_term", [P, B])
        hs = [sb(f"hs{i}", [P, ROW]) for i in range(2)]
        ys = sb("ys", [P, ROW])
        h2 = sb("h2", [P, TILES, P])
        h3 = [sb(f"h3_{i}", [P, TILES, P]) for i in range(2)]
        z3 = sb("z3", [P, TILES, P])
        z3f = sb("z3f", [P, ROW])
        hr = [sb(f"hr{i}", [P, SIDE, 2, B]) for i in range(2)]
        hparts = [sb(f"hparts{i}", [P, 3, 2, B], BF16) for i in range(2)]
        rest = sb("rest", [P, 2, B])
        os_ = sb("os", [P, ROW])
        zh = [sb(f"zh{i}", [P, TILES, WIDE]) for i in range(2)]
        z5f = sb("z5f", [P, ROW])
        lg = sb("lg", [P, TILES, NE])
        lmax = sb("lmax", [P, TILES])
        onehot = sb("onehot", [P, TILES, NE], BF16)
        place = sb("place", [P, TILES, NE])
        placef = sb("placef", [P, TILES])
        placeu = [sb(f"placeu{i}", [P, TILES], U32) for i in range(2)]
        pad = sb("pad", [P, MT, WIDE])
        tilex = sb("tilex", [1, NTILES, NE])
        tab = {n: t[0:1, 0:NTILES * NE].rearrange("p (t e) -> p t e", e=NE)
               for n, t in (("a", gate), ("b", inp))}
        row8 = {n: sb("row8_" + n, [1, NE]) for n in ("count", "tiles", "ends", "starts", "one")}
        row8i = sb("row8i", [1, NE], I32)
        tilef = {n: sb("tilef_" + n, [1, NTILES]) for n in ("place", "any")}
        tileu = sb("tileu", [1, NTILES], U32)
        freeu = sb("freeu", [1, NE], U32)
        flat = [xs[i][:].rearrange("p k n -> p (k n)") for i in range(2)]
        rows = [flat[0][:, i * MT * WIDE:(i + 1) * MT * WIDE].rearrange("p (m f) -> p m f", f=WIDE)
                for i in range(NBUF)]
        wexp = [flat[1][:, i * WEXP:(i + 1) * WEXP] for i in range(NBUF)]
        fin = [(h1[0], h1[1], tokT)[i // 3][:, i % 3 * MT:(i % 3 + 1) * MT, :]
               for i in range(NFIN)]
        after = NBUF * WEXP
        hid = [flat[1][:, after + i * 2 * TS:after + (i + 1) * 2 * TS].rearrange(
            "p (m f) -> p m f", m=2) for i in range(2)]
        zt = [z1f[:, i * TS:(i + 1) * TS] for i in range(2)]
        yt = [ys[:, i * TS:(i + 1) * TS] for i in range(2)]
        fid = [sb(f"fid{i}", [P, MT], U32) for i in range(NFIN)]
        stats = {k: sb("stats_" + k, [P, TILES, 6]) for k in ("tok", "h1", "h2", "h4")}
        mv = {k: sb("mv_" + k, [P, TILES, 2]) for k in ("tok", "h1", "h2", "h4")}
        veps = {k: sb("veps_" + k, [P, TILES]) for k in ("tok", "h1", "h2", "h4", "h3")}
        minus_mean = {k: sb("minus_mean_" + k, [P, TILES]) for k in ("tok", "h1", "h2", "h4")}
        scale = {k: sb("scale_" + k, [P, TILES]) for k in ("tok", "h1", "h2", "h4", "h3")}
        shift = {k: sb("shift_" + k, [P, TILES]) for k in ("tok", "h1", "h2", "h4", "h3")}
        rstd = {k: sb("rstd_" + k, [P, TILES]) for k in ("h2", "h3")}
        one7, eps7 = sb("one7", [P, TILES]), sb("eps7", [P, TILES])
        scratch = sb("scratch", [P, 1])
        carrier = sb("carrier", [P, 3])

        bank = [psum(f"bank{i}") for i in range(GENERAL)]
        pbank = [psum(f"pbank{i}") for i in range(2)]
        rbank = [psum(f"rbank{i}") for i in range(2)]
        wtok_in = sem("wtok_in")
        weights_in = sem("weights_in")
        zeroed = sem("zeroed")
        consts_done = sem("consts_done")
        x_in = [[sem(f"x_in{i}_{c}") for c in range(2)] for i in range(2)]
        shifts_in = [sem("shifts_in0"), sem("shifts_in1")]
        did = {p: sem("did_" + p) for p in PER_ROW}
        left = {p: sem("left_" + p) for p in PER_ROW}
        tok_done = sem("tok_done")
        stepped = sem("stepped")
        part_done = [sem(f"part_done{i}") for i in range(3)]
        rest_done = sem("rest_done")
        kept = sem("kept")
        clipped, decayed = sem("clipped"), sem("decayed")
        split_done = sem("split_done")
        bparts_in = sem("bparts_in")
        xp_done = sem("xp_done")
        v = {n: sem("v_" + n) for n in ("logits", "place")}
        stats_done = {k: sem("stats_done_" + k) for k in ("tok", "h1", "h2", "h4")}
        moments_done = {k: sem("moments_" + k) for k in ("tok", "h1", "h2", "h4")}
        scaled = {k: sem("scaled_" + k) for k in ("tok", "h1", "h2", "h4")}
        affine = sem("affine")
        n1_done, z1_done, z3_done, h3_done, z5_done = (
            sem(n + "_done") for n in ("n1", "z1", "z3", "h3", "z5"))
        scattered = [sem("scattered0"), sem("scattered1")]
        ends_known, tables_done, pads_in = sem("ends_known"), sem("tables_done"), sem("pads_in")
        tile_in = [sem(f"tile_in{i}") for i in range(NBUF)]
        t_z, t_zt, t_h, t_hid, t_hid1, t_y, t_yt, t_o, t_fin = (
            sem("t_" + n) for n in ("z", "zt", "h", "hid", "hid1", "y", "yt", "o", "fin"))
        out_done = [sem(f"out_done{i}") for i in range(NFIN)]
        scan_done = sem("scan_done")
        dve_chain, pool_chain = sem("dve_chain"), sem("pool_chain")
        t_ids = sem("t_ids")
        t_carried = sem("t_carried")
        scratched = sem("scratched")
        carried = sem("carried")

        def wv(i):
            return vec[:, i:i + 1]

        def slot(eng, s, piece, before_step):
            if not s.valid():
                for name in stepless_order():
                    piece(s, name)
                return
            for j, group in enumerate(PLAN):
                before_step(s, j)
                for name in group:
                    piece(s, name)

        def all_slots(eng, piece, step, before=lambda: None, steady=lambda: None):
            for n in range(-4, LOOP[0] + 1):
                slot(eng, Row(0, n), piece, step)
            before()
            with eng.Fori(LOOP[0], LOOP[1] - 1, 2) as base:
                for n in range(2):
                    slot(eng, Row(base, n + 1), piece, step)
                steady()
            for n in range(LOOP[1] + 1, SIDE + 1):
                slot(eng, Row(0, n), piece, step)

        def write_pads(eng, some):
            eng.wait_ge(ends_known, 1)
            for e in some:
                at = eng.value_load(freeu[0:1, e:e + 1], min_val=0, max_val=NE * CAP - TS)
                eng.dma_start(places[bass.ds(at, TS), :].rearrange("(p m) f -> p m f", m=MT),
                              pad[:]).then_inc(pads_in, 16)

        block = ctx.enter_context(nc.Block())

        @block.sync
        def _(sp):
            def load_patches(par, row):
                for c in range(2):
                    cols = slice(c * HALF, (c + 1) * HALF)
                    sp.dma_start(xs[par][:, :, cols], x[row][:, :, cols])\
                        .then_inc(x_in[par][c], 16)

            sp.dma_start(wtok[:], w_tok).then_inc(wtok_in, 16)
            load_patches(0, 0)
            for dst, src in [(wattn, w_attn), (vec, vectors), (gb, rows_gb), (wih, w_ih),
                             (whh, w_hh), (wout, w_out), (brow, b_rnn), (wgate, w_gate),
                             (bgate, b_gate), (eye, ident), (ids, first_ids), (tri32, triangle)]:
                sp.dma_start(dst[:], src).then_inc(weights_in, 16)
            load_patches(1, 1)
            sp.wait_ge(split_done, 1)
            for i in range(3):
                sp.dma_start(bparts[i:i + 1, :], bsplit[0:1, i, :]).then_inc(bparts_in, 16)
            sp.wait_ge(consts_done, 1)

            def piece(s, name):
                if name == "xp1":
                    nxt = s.shift(5)
                    if nxt.valid() and not nxt.early():
                        sp.wait_ge(did["project1"], nxt.count(1, -1))
                        load_patches(nxt.par, nxt.index())
                if name == "finish_tok":
                    f, nxt = s.shift(2), s.shift(3)
                    if f.valid():
                        dst, mine = sh[f.par], yp[f.par]
                        if f.first():
                            sp.wait_ge(left["project1"], f.count(1, 1))
                        elif nxt.valid():
                            sp.wait_ge(left["project1"], nxt.count(1, 1))
                        if f.first():
                            sp.dma_start(dst[112:128, :], zeros[0:16, :]).then_inc(shifts_in[0], 16)
                        s_in = shifts_in[f.par]
                        sp.dma_start(dst[64:80, 0:PADDED - 1], mine[80:96, 2:]).then_inc(s_in, 16)
                        sp.dma_start(dst[80:96, :], mine[64:80, 0:PADDED]).then_inc(s_in, 16)
                        if f.first():
                            sp.wait_ge(left["project1"], nxt.count(1, 1))
                        below = yp[nxt.par][112:128, 1:] if nxt.valid() else zeros[0:16, :]
                        sp.dma_start(dst[96:112, :], below).then_inc(s_in, 16)
                        if nxt.valid():
                            if not f.first():
                                sp.wait_ge(tok_done, f.count(1, 0))
                            sp.dma_start(sh[nxt.par][112:128, :], mine[96:112, 1:])\
                                .then_inc(shifts_in[nxt.par], 16)
            all_slots(sp, piece, lambda s, j: None)

            write_pads(sp, range(0, NE, 2))
            sp.wait_ge(tables_done, 1)

            def first_place(t):
                return sp.value_load(tileu[0:1, bass.ds(t, 1)], min_val=0, max_val=NE * CAP - TS)

            def load_rows(i, at):
                sp.dma_start(rows[i][:], places[bass.ds(at, TS), :].rearrange(
                    "(p m) f -> p m f", m=MT)).then_inc(tile_in[i], 16)

            def load_weights(i, at):
                sp.dma_start(wexp[i][:], experts[bass.ds(at // CAP, 1), :, :].rearrange(
                    "e p w -> (e p) w")).then_inc(tile_in[i], 16)

            early = 2
            for i in range(early):
                load_weights(i, first_place(i))
            at = first_place(0)
            sp.wait_ge(pads_in, 16 * NE)
            for i in range(2):
                sp.wait_ge(scattered[i], 16 * TILES * SIDE // 2)
            load_rows(0, at)
            for i in range(1, NBUF):
                at = first_place(i)
                load_rows(i, at)
                if i >= early:
                    load_weights(i, at)
            with sp.Fori(NBUF, NTILES - NBUF + 1, NBUF) as t:
                for i in range(NBUF):
                    sp.wait_ge(t_fin, t + (i - NBUF + 1))
                    at = first_place(t + i)
                    load_rows(i, at)
                    load_weights(i, at)

        @block.tensor
        def _(pe):
            pe.wait_ge(wtok_in, 16)

            def claim(s, name, job):
                t = [turn[:2] for turn in TURNS].index((name, job))
                before = [(s, b) for b in range(t - GENERAL, -1, -GENERAL)]
                before += [(s.shift(-1), b) for b in reversed(range(len(TURNS)))
                           if b % GENERAL == t % GENERAL]
                for at, b in before:
                    p, j, off = TURNS[b]
                    if at.shift(off).valid():
                        pe.wait_ge(left[p], at.shift(off).count(PER_ROW[p], j + 1))
                        break
                return bank[t % GENERAL]

            def transposes(s, r, name, src, ready=None):
                for c, (a, b) in enumerate(SPANS[name]):
                    if ready is not None:
                        pe.wait_ge(ready, r.count(2, c + 1))
                    dst = claim(s, name, c)
                    for m in range(a, b):
                        ins = pe.transpose(dst[:, (m - a) * P:(m - a + 1) * P], src(m), eye[:])
                    ins.then_inc(did[name], 1)

            def piece(s, name):
                u, w, v_, d = s.shift(1), s.shift(-1), s.shift(4), s.shift(2)
                if name.startswith("project") and v_.valid():
                    c, part = int(name[7]), "abc".index(name[8])
                    if part == 0 and not v_.first():
                        pe.wait_ge(left[name[:8]], v_.count(1, 0))
                    if part == 0:
                        pe.wait_ge(x_in[v_.par][c], v_.pair_count(16))
                    for k in range(part * KC // 3, (part + 1) * KC // 3):
                        ins = pe.matmul(pbank[c][:, 0:HALF], wtok[:, k, :],
                                        xs[v_.par][:, k, c * HALF:(c + 1) * HALF],
                                        start=(k == 0), stop=(k == KC - 1))
                    if part == 2:
                        ins.then_inc(did[name[:8]], 1)
                if name == "d" and d.valid():
                    if d.first():
                        pe.wait_ge(weights_in, 16 * 12)
                        pe.wait_ge(consts_done, 1)
                        pe.wait_ge(bparts_in, 48)
                    pe.wait_ge(tok_done, d.count(1, 1))
                    transposes(s, d, "d", lambda m: tok[d.par][:, m * P:(m + 1) * P])
                if name.startswith("xp"):
                    inputs_of_group(s if name != "xp0" else u, int(name[2]))
                if name == "e" and u.valid():
                    transposes(s, u, "e", lambda m: z1[:, m, :], z1_done)
                if name in ("gates0", "gates1") and u.valid():
                    c = int(name[5])
                    pe.wait_ge(left["e"], u.count(2, c + 1))
                    for i, kind in enumerate(("sigmoid", "inputs")):
                        dst = claim(s, kind, c)
                        pe.matmul(dst[:, 0:HALF], wattn[:, i, :],
                                  z1f[:, c * HALF:(c + 1) * HALF], start=True, stop=True)\
                            .then_inc(did[kind], 1)
                if name in ("y0", "y1") and u.valid():
                    c = int(name[1])
                    dst = claim(s, "y", c)
                    pe.matmul(dst[:, 0:HALF], wattn[:, 3, :], z1f[:, c * HALF:(c + 1) * HALF],
                              start=True, stop=False)
                    if c == 0:
                        pe.wait_ge(scan_done, u.count(1, 1))
                    pe.matmul(dst[:, 0:HALF], wattn[:, 2, :],
                              hs[u.par][:, c * HALF:(c + 1) * HALF],
                              start=False, stop=True).then_inc(did["y"], 1)
                if name == "h2" and u.valid():
                    transposes(s, u, "h2", lambda m: ys[:, m * P:(m + 1) * P], left["y"])
                if name == "z3" and u.valid():
                    transposes(s, u, "z3", lambda m: z3[:, m, :], z3_done)
                if name in ("o0", "o1") and w.valid():
                    c = int(name[1])
                    pe.wait_ge(kept, w.count(4, 4))
                    dst = claim(s, "o", c)
                    for k in range(2):
                        states = hr[w.par][:, :, k, c * B // 2:(c + 1) * B // 2]\
                            .rearrange("p j b -> p b j")
                        ins = pe.matmul(dst[:, 0:HALF], wout[:, k, :], states,
                                        start=(k == 0), stop=(k == 1))
                    ins.then_inc(did["o"], 1)
                if name == "h4" and w.valid():
                    transposes(s, w, "h4", lambda m: os_[:, m * P:(m + 1) * P], left["o"])
                if name == "z5" and w.valid():
                    transposes(s, w, "z5", lambda m: zh[w.par][:, m, 0:P], z5_done)
                if name == "logits" and w.valid():
                    dst = claim(s, name, 0)
                    for m in range(TILES):
                        for c, (a, b) in enumerate(SPANS["z5"]):
                            if m == a:
                                pe.wait_ge(left["z5"], w.count(2, c + 1))
                        ins = pe.matmul(dst[:, m * NE:(m + 1) * NE],
                                        z5f[:, m * P:(m + 1) * P], wgate[:],
                                        start=True, stop=True)
                    ins.then_inc(did[name], 1)
                if name == "prefix" and w.valid():
                    pe.wait_ge(v["logits"], w.count(1, 1))
                    dst = claim(s, name, 0)
                    wide = TILES * NE
                    chosen = onehot[:].rearrange("p m e -> p (m e)")
                    pe.matmul(dst[:, 0:wide], tri[:], chosen, start=True, stop=False,
                              skip_group_check=True)
                    for back in range(1, TILES):
                        pe.matmul(dst[:, back * NE:wide], ones[:], chosen[:, 0:wide - back * NE],
                                  start=False, stop=False, skip_group_check=True)
                    for m in range(TILES):
                        ins = pe.matmul(dst[:, wide:wide + NE], ones[:],
                                        chosen[:, m * NE:(m + 1) * NE],
                                        start=False, stop=(m == TILES - 1), skip_group_check=True)
                    ins.then_inc(did[name], 1)

            def inputs_of_group(r, g):
                if not r.valid():
                    return
                steps = steps_of(g)
                n = len(steps)
                if g == 0:
                    pe.wait_ge(left["z3"], r.count(2, 2))
                if not r.first() or g >= 2:
                    pe.wait_ge(kept, r.count(4, g - 1))
                inputs = z3f[:].rearrange("p (b j) -> p j b", j=SIDE)[:, steps[0]:steps[-1] + 1:2, :]
                at = rbank[g % 2][:].rearrange("p (j m b) -> p j m b", m=2, b=B)
                for m in range(2):
                    pe.matmul(at[:, 0:n, m, :], wih[:, m, :], inputs,
                              start=(m == 0), stop=False, skip_group_check=True)
                for m in range(2):
                    ins = pe.matmul(at[:, 0:n, m, :], bparts[:, m * P:(m + 1) * P],
                                    ones3[:, 0:n * B].rearrange("p (j b) -> p j b", b=B),
                                    start=False, stop=True, skip_group_check=True)
                ins.then_inc(xp_done, 1)

            def step(s, j):
                if s.first() and j == 0:
                    return
                base = (j % (2 * GROUP)) // 2 * 2 * B
                for part in range(3):
                    pe.wait_ge(part_done[part], s.count(SIDE, j))
                    for m in range(2):
                        for k in range(2):
                            for other in range(3 - part):
                                ins = pe.matmul(
                                    rbank[j % 2][:, base + m * B:base + (m + 1) * B],
                                    whhp[other][:, k, m, :],
                                    hparts[(j + 1) % 2][:, part, k, :],
                                    start=False, stop=True, skip_group_check=True)
                ins.then_inc(stepped, 1)

            all_slots(pe, piece, step)

            def turn(t, i, z, mid, y):
                if mid is not None:
                    pe.wait_ge(t_zt, t + 1)
                    if not mid:
                        pe.wait_ge(t_hid, t)
                        pe.wait_ge(t_hid1, t)
                    for m in range(2):
                        pe.matmul(pbank[m][:, 0:TS], wexp[i][:, m * P:(m + 1) * P], zt[i % 2][:],
                                  start=True, stop=True).then_inc(t_h, 1)
                if z is not None:
                    n = (i + 1) % NBUF
                    pe.wait_ge(tile_in[n], z)
                    if mid is not None and not mid:
                        pe.wait_ge(t_zt, t)
                    for m in range(MT):
                        ins = pe.transpose(bank[n % 2][:, m * P:(m + 1) * P],
                                           rows[n][:, m, 0:P], eye[:])
                    ins.then_inc(t_z, 1)
                if y:
                    k = (i + 1) % 2
                    pe.wait_ge(t_yt, t)
                    if y != "first":
                        pe.wait_ge(t_fin, t - 2)
                    for m in range(MT):
                        ins = pe.transpose(rbank[k][:, m * P:(m + 1) * P],
                                           yt[k][:, m * P:(m + 1) * P], eye[:])
                    ins.then_inc(t_o, 1)
                if mid is not None:
                    for m in range(2):
                        pe.wait_ge((t_hid, t_hid1)[m], t + 1)
                        ins = pe.matmul(bank[2 + i % 2][:, 0:TS],
                                        wexp[i][:, (2 + m) * P:(3 + m) * P], hid[i % 2][:, m, :],
                                        start=(m == 0), stop=(m == 1))
                    ins.then_inc(t_y, 1)

            turn(-1, NBUF - 1, 32, None, None)
            for t in range(NBUF):
                turn(t, t, 32 * ((t + 1) // NBUF + 1), t == 0, (None, "first", "y")[min(t, 2)])
            with pe.Fori(NBUF, NTILES - 2 * NBUF + 1, NBUF) as t:
                for i in range(NBUF):
                    turn(t + i, i, t * (32 // NBUF) + 32 * ((i + 1) // NBUF + 1), False, "y")
            for t in range(NTILES - NBUF, NTILES):
                turn(t, t % NBUF, 32 * ((t + 1) // NBUF + 1) if t + 1 < NTILES else None,
                     False, "y")
            turn(NTILES, 0, None, None, "y")

        @block.scalar
        def _(act):
            act.wait_ge(weights_in, 16 * 12)
            act.wait_ge(zeroed, 1)

            def leave(r, name, job, dst, src, func=ACT.Identity, **kw):
                act.wait_ge(did[name], r.count(PER_ROW[name], job + 1))
                nc.scalar.activation(dst, src, func, **kw).then_inc(left[name], 1)

            def turn_bank(name, job):
                return bank[bank_of(name, job)]

            def leave_transposes(r, name, dst):
                for c, (a, b) in enumerate(SPANS[name]):
                    leave(r, name, c, dst(a, b), turn_bank(name, c)[:, 0:(b - a) * P])

            def normalise(dst, src, key, done=None, name=None):
                for m in range(TILES):
                    ins = nc.scalar.activation(dst[:, m, 0:P], src[:, m, :], ACT.Identity,
                                               bias=shift[key][:, m:m + 1],
                                               scale=scale[key][:, m:m + 1])
                    if name and m + 1 in (b for a, b in SPANS[name]):
                        ins.then_inc(done, 1)
                return ins

            def piece(s, name):
                u, w, v_, d = s.shift(1), s.shift(-1), s.shift(4), s.shift(2)
                if name.startswith("project") and name[8] == "c" and v_.valid():
                    c, name = int(name[7]), name[:8]
                    src = pbank[c]
                    act.wait_ge(did[name], v_.count(1, 1))
                    if c == 0 and not v_.early():
                        act.wait_ge(tok_done, v_.count(1, -1))
                        act.wait_ge(shifts_in[(v_.par + 1) % 2], v_.shift(-1).pair_count(64) - 48)
                        act.wait_ge(did["d"], v_.count(2, -2))
                    nc.scalar.activation(tok[v_.par][0:64, c * HALF:(c + 1) * HALF],
                                         src[0:64, 0:HALF], ACT.Identity, bias=vec[0:64, 0:1])
                    dst = yp[v_.par][64:128, 1:].rearrange("p (b j) -> p b j", j=SIDE + 1)[
                        :, c * B // 2:(c + 1) * B // 2, 0:SIDE]
                    nc.scalar.activation(dst, src[64:128, 0:HALF].rearrange(
                        "p (b j) -> p b j", j=SIDE), ACT.Identity).then_inc(left[name], 1)
                if name == "d" and d.valid():
                    leave_transposes(d, "d", lambda a, b: tokT[:, a:b, :])
                if name == "e" and u.valid():
                    leave_transposes(u, "e", lambda a, b: z1f[:, a * P:b * P])
                if name in ("gates0", "gates1") and u.valid():
                    c = int(name[5])
                    leave(u, "sigmoid", c, gate[:, c * HALF:(c + 1) * HALF],
                          turn_bank("sigmoid", c)[:, 0:HALF], ACT.Sigmoid)
                if name in ("y0", "y1") and u.valid():
                    c = int(name[1])
                    leave(u, "y", c, ys[:, c * HALF:(c + 1) * HALF],
                          turn_bank("y", c)[:, 0:HALF], bias=byscaled[:, 0:1], scale=HSCALE)
                if name in ("open0", "open1") and u.valid():
                    c = int(name[4])
                    cols = slice(c * HALF, (c + 1) * HALF)
                    act.wait_ge(clipped, u.count(2, c + 1))
                    nc.scalar.activation(decay[:, cols], gate[:, cols], ACT.Identity, bias=1.0,
                                         scale=a_minus_1[:, 0:1]).then_inc(decayed, 1)
                if name.startswith("keep") and s.valid():
                    g = int(name[4])
                    steps = steps_of(g)
                    act.wait_ge(rest_done, s.count(SIDE, steps[-1] + 1))
                    if g == 0 and not s.early():
                        act.wait_ge(did["o"], s.count(2, -2))
                    nc.scalar.activation(
                        hr[s.par][:, steps[0]:steps[-1] + 1:2, :, :],
                        rbank[g % 2][:, 0:len(steps) * 2 * B].rearrange(
                            "p (j m b) -> p j m b", m=2, b=B), ACT.Relu).then_inc(kept, 1)
                if name == "n1" and d.valid():
                    act.wait_ge(scaled["tok"], d.count(1, 1))
                    normalise(h1[d.par], tokT, "tok").then_inc(n1_done, 1)
                if name == "z1n" and d.valid():
                    act.wait_ge(scaled["h1"], d.count(1, 1))
                    if not d.first():
                        act.wait_ge(did["e"], d.count(2, 0))
                    normalise(z1, h1[d.par], "h1", z1_done, "e")
                if name == "z3n" and u.valid():
                    act.wait_ge(scaled["h2"], u.count(1, 1))
                    if not u.first():
                        act.wait_ge(did["z3"], u.count(2, 0))
                    normalise(z3, h2, "h3", z3_done, "z3")
                if name == "h3n" and s.valid():
                    if not s.early():
                        act.wait_ge(left["h4"], s.count(2, -2))
                    normalise(h3[s.par], h2, "h2").then_inc(h3_done, 1)
                if name == "z5n" and w.valid():
                    act.wait_ge(scaled["h4"], w.count(1, 1))
                    mine = zh[w.par]
                    normalise(mine, mine[:, :, P:2 * P], "h4", z5_done, "z5")
                if name == "z3" and u.valid():
                    if not u.first():
                        act.wait_ge(xp_done, u.count(4, 0))
                    leave_transposes(u, "z3", lambda a, b: z3f[:, a * P:b * P])
                if name in ("o0", "o1") and w.valid():
                    c = int(name[1])
                    leave(w, "o", c, os_[:, c * HALF:(c + 1) * HALF],
                          turn_bank("o", c)[:, 0:HALF], bias=wv(V_BO))
                if name == "z5" and w.valid():
                    leave_transposes(w, "z5", lambda a, b: z5f[:, a * P:b * P])
            all_slots(act, piece, lambda s, j: None)
            write_pads(act, range(1, NE, 2))

            def tile_z(t, n, first):
                act.wait_ge(t_z, t + 1)
                if not first:
                    act.wait_ge(t_h, 2 * (t - 1))
                nc.scalar.activation(zt[n % 2][:], bank[n % 2][:, 0:TS], ACT.Identity)\
                    .then_inc(t_zt, 1)

            def tile_hidden(t, i, first):
                act.wait_ge(t_h, 2 * t + 1)
                if not first:
                    act.wait_ge(t_y, t - 1)
                nc.scalar.activation(hid[i % 2][:, 0, :], pbank[0][:, 0:TS], ACT.Relu,
                                     bias=wexp[i][:, 4 * P:4 * P + 1]).then_inc(t_hid, 1)

            def tile_y(t, i, first):
                act.wait_ge(t_y, t + 1)
                if not first:
                    act.wait_ge(t_o, t - 1)
                nc.scalar.activation(yt[i % 2][:], bank[2 + i % 2][:, 0:TS], ACT.Identity,
                                     bias=wexp[i][:, 4 * P + 2:4 * P + 3]).then_inc(t_yt, 1)

            tile_z(0, 0, True)
            for t in range(NBUF):
                tile_hidden(t, t, t < 2)
                tile_z(t + 1, t + 1, t + 1 < 2)
                tile_y(t, t, t < 2)
            with act.Fori(NBUF, NTILES - 2 * NBUF + 1, NBUF) as t:
                for i in range(NBUF):
                    tile_hidden(t + i, i, False)
                    tile_z(t + i + 1, i + 1, False)
                    tile_y(t + i, i, False)
            for t in range(NTILES - NBUF, NTILES):
                tile_hidden(t, t % NBUF, False)
                if t + 1 < NTILES:
                    tile_z(t + 1, t + 1, False)
                tile_y(t, t % NBUF, False)

        @block.gpsimd
        def _(pool):
            links = [0]

            def link(ins, s):
                links[0] += 1
                ins.then_inc(pool_chain, 1)
                if isinstance(s.base, int):
                    pool.wait_ge(pool_chain, links[0])
                else:
                    pool.wait_ge(pool_chain, (s.base - LOOP[0]) * POOL_LINKS + links[0])

            links_before = [0]

            def steady():
                turns = (LOOP[1] - LOOP[0]) // 2
                assert links[0] - links_before[0] == 2 * POOL_LINKS, links[0] - links_before[0]
                links[0] += (turns - 1) * 2 * POOL_LINKS

            pool.wait_ge(weights_in, 16 * 12)
            pool.wait_ge(consts_done, 1)

            def carry(cell=0, count=carried, by=1):
                nc.gpsimd.tensor_tensor(carrier[:, cell:cell + 1], carrier[:, 2:3],
                                        carrier[:, 2:3], ALU.add).then_inc(count, by)

            def small(dst, a, b, op):
                return nc.gpsimd.tensor_tensor(dst[:], a[:], b[:], op)

            def scale_and_shift(s, r, key):
                pool.wait_ge(moments_done[key], r.count(1, 1))
                link(small(scale[key], veps[key], minus_half, ALU.pow), s)
                small(shift[key], minus_mean[key], scale[key], ALU.mult).then_inc(scaled[key], 1)

            def piece(s, name):
                u, w, d = s.shift(1), s.shift(-1), s.shift(2)
                if name == "tok_mv" and d.valid():
                    scale_and_shift(s, d, "tok")
                if name == "n1" and d.valid():
                    g = gb[:, 0, :].unsqueeze(1).broadcast_to([P, TILES, P])
                    b = gb[:, 1, :].unsqueeze(1).broadcast_to([P, TILES, P])
                    pool.wait_ge(n1_done, d.count(1, 1))
                    mine = h1[d.par][:]
                    nc.gpsimd.tensor_tensor(mine, mine, g, ALU.mult).then_inc(affine, 1)
                    pool.wait_ge(affine, d.count(2, 1))
                    nc.gpsimd.tensor_tensor(mine, mine, b, ALU.add).then_inc(affine, 1)
                if name == "h1_mv" and d.valid():
                    scale_and_shift(s, d, "h1")
                if name == "h2_mv" and u.valid():
                    pool.wait_ge(moments_done["h2"], u.count(1, 1))
                    link(small(rstd["h2"], veps["h2"], minus_half, ALU.pow), s)
                    link(small(scale["h2"], rstd["h2"], one7, ALU.add), s)
                    link(small(veps["h3"], scale["h2"], scale["h2"], ALU.mult), s)
                    link(nc.gpsimd.tensor_tensor(veps["h3"][:], veps["h3"][:], mv["h2"][:, :, 1],
                                                 ALU.mult), s)
                    link(small(veps["h3"], veps["h3"], eps7, ALU.add), s)
                    link(small(rstd["h3"], veps["h3"], minus_half, ALU.pow), s)
                    link(small(scale["h3"], scale["h2"], rstd["h3"], ALU.mult), s)
                    small(shift["h2"], minus_mean["h2"], rstd["h2"], ALU.mult)
                    small(shift["h3"], minus_mean["h2"], scale["h3"], ALU.mult)\
                        .then_inc(scaled["h2"], 1)
                if name == "h4_mv" and w.valid():
                    scale_and_shift(s, w, "h4")
                if name == "place" and w.valid():
                    pool.wait_ge(v["place"], w.count(1, 1))
                    carry()
                    for m in range(TILES):
                        nc.gpsimd.indirect_dma_start(
                            places, bass.IndirectOffsetOnAxis(ap=placeu[w.par][:, m:m + 1], axis=0),
                            zh[w.par][:, m, :], None, bounds_check=NE * CAP - 1,
                            oob_is_err=False).then_inc(scattered[w.par], 16)

            all_slots(pool, piece, lambda s, j: None,
                      lambda: links_before.append(links_before.pop() + links[0]), steady)

            def tiles_out(t, i):
                pool.wait_ge(t_fin, t + 2)
                if not isinstance(t, int) or t:
                    pool.wait_ge(t_carried, t)
                carry(1, t_carried, 2)
                for n in (i, i + 1):
                    for m in range(MT):
                        nc.gpsimd.indirect_dma_start(
                            out, bass.IndirectOffsetOnAxis(ap=fid[n][:, m:m + 1], axis=0),
                            fin[n][:, m, :], None, bounds_check=TOKENS - 1,
                            oob_is_err=False).then_inc(out_done[n], 16)

            for i in range(0, NFIN, 2):
                tiles_out(i, i)
            with pool.Fori(NFIN, NTILES - NFIN + 1, NFIN) as t:
                for i in range(0, NFIN, 2):
                    tiles_out(t + i, i)
            for i in range(NFIN):
                pool.wait_ge(out_done[i], 16 * MT * NTILES // NFIN)

        @block.vector
        def _(dve):
            links = [0]

            def link(ins, s=Row(0, 0), wait=True):
                links[0] += 1
                ins.then_inc(dve_chain, 1)
                if not wait:
                    return
                if isinstance(s.base, int):
                    dve.wait_ge(dve_chain, links[0])
                else:
                    dve.wait_ge(dve_chain, (s.base - LOOP[0]) * LINKS + links[0])

            link(dve.memset(zeros[:], 0.0))
            for i in range(2):
                link(dve.memset(yp[i][:], 0.0))
            dve.sem_inc(zeroed, 1)
            link(dve.memset(one7[:], 1.0))
            link(dve.memset(eps7[:], EPS))
            link(dve.memset(minus_half[:], -0.5))
            link(dve.memset(ones[:], 1.0))
            link(dve.memset(carrier[:], 0.0))
            link(dve.memset(ones3[:], 1.0))
            link(dve.memset(row8["one"][:], 1.0))
            link(dve.memset(pad[:], 0.0))
            link(dve.memset(pad[:, :, 2 * P:2 * P + 1], NOWHERE))
            for i in range(2):
                link(dve.memset(zh[i][:, :, 2 * P:WIDE], 0.0))
            for e in range(NE):
                link(dve.memset(rank[:, e:e + 1], float(NE - e)))
                link(dve.memset(region[:, e:e + 1], float(e * CAP)))
            for t in range(NTILES):
                ins = dve.memset(tilex[:, t, :], float(t))
            link(ins)
            link(dve.tensor_copy(free[:], region[:]))
            dve.wait_ge(weights_in, 16 * 12)
            link(dve.tensor_tensor(brow[:, 0, :], brow[:, 0, :], brow[:, 1, :], ALU.add))
            for i in range(3):
                link(dve.tensor_copy(bsplit[:, i, :], brow[:, 0, :]))
                link(dve.tensor_tensor(brow[:, 0, :], brow[:, 0, :], bsplit[:, i, :],
                                       ALU.subtract))
                link(dve.tensor_copy(whhp[i][:], whh[:]))
                link(dve.tensor_tensor(whh[:], whh[:], whhp[i][:], ALU.subtract))
            dve.sem_inc(split_done, 1)
            link(dve.tensor_copy(tri[:], tri32[:]))
            link(dve.tensor_scalar(byscaled[:], wv(V_BY), HSCALE, None, ALU.mult))
            link(dve.tensor_scalar(a_minus_1[:], wv(V_A), -1.0, None, ALU.add))
            dve.sem_inc(consts_done, 1)

            def turn_bank(name, job):
                return bank[bank_of(name, job)]

            links_before = [0]

            def steady():
                turns = (LOOP[1] - LOOP[0]) // 2
                assert links[0] - links_before[0] == 2 * LINKS, links[0] - links_before[0]
                links[0] += (turns - 1) * 2 * LINKS

            def statistics(key, src):
                for m in range(TILES):
                    ins = dve.bn_stats(stats[key][:, m, :], src[:, m, :])
                ins.then_inc(stats_done[key], 1)

            def moments(s, r, key):
                dve.wait_ge(stats_done[key], r.count(1, 1))
                dve.memset(scratch[:], 0.0).then_inc(scratched, 1)
                for m in range(TILES):
                    ins = dve.bn_aggr(mv[key][:, m, :], stats[key][:, m, :])
                link(ins, s)
                dve.tensor_scalar(minus_mean[key][:], mv[key][:, :, 0], -1.0, None, ALU.mult)
                dve.tensor_scalar(veps[key][:], mv[key][:, :, 1], EPS, None, ALU.add)\
                    .then_inc(moments_done[key], 1)

            def piece(s, name):
                u, w, d = s.shift(1), s.shift(-1), s.shift(2)
                if name == "finish_tok" and d.valid():
                    dve.wait_ge(shifts_in[d.par], d.pair_count(64))
                    dve.wait_ge(left["project1"], d.count(1, 1))
                    if not d.early():
                        dve.wait_ge(did["d"], d.count(2, -2))
                    own = yp[d.par][64:128, 1:].rearrange("p (b j) -> p b j", j=SIDE + 1)
                    other = sh[d.par][64:128, :].rearrange("p (b j) -> p b j", j=SIDE + 1)
                    dve.scalar_tensor_tensor(
                        tok[d.par][64:128, :].rearrange("p (b j) -> p b j", j=SIDE),
                        own[:, :, 0:SIDE], vec[64:128, 0:1], other[:, :, 0:SIDE],
                        ALU.add, ALU.add).then_inc(tok_done, 1)
                if name == "tok_stats" and d.valid():
                    dve.wait_ge(left["d"], d.count(2, 2))
                    statistics("tok", tokT)
                if name == "tok_mv" and d.valid():
                    moments(s, d, "tok")
                if name == "h1_stats" and d.valid():
                    dve.wait_ge(affine, d.count(2, 2))
                    statistics("h1", h1[d.par])
                if name == "h1_mv" and d.valid():
                    moments(s, d, "h1")
                if name in ("open0", "open1") and u.valid():
                    c = int(name[4])
                    cols = slice(c * HALF, (c + 1) * HALF)
                    dve.wait_ge(left["sigmoid"], u.count(2, c + 1))
                    dve.tensor_scalar(gate[:, cols], gate[:, cols], 0.05, 0.95, ALU.max, ALU.min)\
                        .then_inc(clipped, 1)
                    dve.wait_ge(clipped, u.count(2, c + 1))
                    dve.wait_ge(did["inputs"], u.count(2, c + 1))
                    dve.scalar_tensor_tensor(inp[:, cols], turn_bank("inputs", c)[:, 0:HALF],
                                             wv(V_BH), gate[:, cols], ALU.add, ALU.mult)\
                        .then_inc(left["inputs"], 1)
                if name == "scan" and u.valid():
                    dve.wait_ge(left["inputs"], u.count(2, 2))
                    dve.wait_ge(decayed, u.count(2, 2))
                    a3 = decay[:].rearrange("p (b j) -> p b j", j=SIDE)
                    b3 = inp[:].rearrange("p (b j) -> p b j", j=SIDE)
                    if not u.first():
                        before = hs[1 - u.par][:].rearrange("p (b j) -> p b j", j=SIDE)
                        link(dve.tensor_tensor(first_term[:], a3[:, :, 0], before[:, :, SIDE - 1],
                                               ALU.mult), s)
                    link(dve.memset(a3[:, :, 0], 0.0), s, wait=u.first())
                    if not u.first():
                        link(dve.tensor_tensor(b3[:, :, 0], b3[:, :, 0], first_term[:], ALU.add), s)
                    if not u.early():
                        dve.wait_ge(did["y"], u.count(2, -2))
                    dve.tensor_tensor_scan(hs[u.par][:], decay[:], inp[:], 0.0, ALU.mult, ALU.add)\
                        .then_inc(scan_done, 1)
                    dve.wait_ge(scan_done, u.count(1, 1))
                if name == "h2_add" and u.valid():
                    if not u.first():
                        dve.wait_ge(h3_done, u.count(1, 0))
                    for c, (a, b) in enumerate(SPANS["h2"]):
                        dve.wait_ge(did["h2"], u.count(2, c + 1))
                        dve.tensor_tensor(h2[:, a:b, :], h1[u.par][:, a:b, :],
                                          turn_bank("h2", c)[:, 0:(b - a) * P].rearrange(
                                              "p (m f) -> p m f", f=P), ALU.add)\
                            .then_inc(left["h2"], 1)
                if name == "h2_stats" and u.valid():
                    dve.wait_ge(left["h2"], u.count(2, 2))
                    statistics("h2", h2)
                if name == "h2_mv" and u.valid():
                    moments(s, u, "h2")
                if name == "h4_add" and w.valid():
                    mine = zh[w.par]
                    if not w.early():
                        dve.wait_ge(scattered[w.par], w.pair_count(16 * TILES) - 16 * TILES)
                    dve.wait_ge(h3_done, w.count(1, 1))
                    for c, (a, b) in enumerate(SPANS["h4"]):
                        dve.wait_ge(did["h4"], w.count(2, c + 1))
                        dve.tensor_tensor(mine[:, a:b, P:2 * P], h3[w.par][:, a:b, :],
                                          turn_bank("h4", c)[:, 0:(b - a) * P].rearrange(
                                              "p (m f) -> p m f", f=P), ALU.add)\
                            .then_inc(left["h4"], 1)
                    link(dve.tensor_copy(mine[:, :, 2 * P], ids[:]), s)
                    link(dve.tensor_scalar(ids[:], ids[:], float(ROW), None, ALU.add), s,
                         wait=False)
                if name == "h4_stats" and w.valid():
                    dve.wait_ge(left["h4"], w.count(2, 2))
                    statistics("h4", zh[w.par][:, :, P:2 * P])
                if name == "h4_mv" and w.valid():
                    moments(s, w, "h4")
                if name == "pick" and w.valid():
                    dve.wait_ge(did["logits"], w.count(1, 1))
                    lg_in = turn_bank("logits", 0)[:, 0:TILES * NE].rearrange(
                        "p (m e) -> p m e", e=NE)
                    dve.tensor_tensor(lg[:], lg_in, bgate[:].unsqueeze(1).broadcast_to(
                        [P, TILES, NE]), ALU.add).then_inc(left["logits"], 1)
                    dve.wait_ge(left["logits"], w.count(1, 1))
                    link(dve.tensor_reduce(lmax[:], lg[:], AX.X, ALU.max), s)
                    link(dve.tensor_tensor(lg[:], lg[:], lmax[:].unsqueeze(2).broadcast_to(
                        [P, TILES, NE]), ALU.is_equal), s)
                    link(dve.tensor_tensor(lg[:], lg[:], rank[:].unsqueeze(1).broadcast_to(
                        [P, TILES, NE]), ALU.mult), s)
                    link(dve.tensor_reduce(lmax[:], lg[:], AX.X, ALU.max), s)
                    if not w.first():
                        dve.wait_ge(did["prefix"], w.count(1, 0))
                    dve.tensor_tensor(onehot[:], lmax[:].unsqueeze(2).broadcast_to(
                        [P, TILES, NE]), rank[:].unsqueeze(1).broadcast_to([P, TILES, NE]),
                        ALU.is_equal).then_inc(v["logits"], 1)
                    dve.wait_ge(v["logits"], w.count(1, 1))
                if name == "place" and w.valid():
                    dve.wait_ge(did["prefix"], w.count(1, 1))
                    src = turn_bank("prefix", 0)
                    wide = TILES * NE
                    link(dve.tensor_tensor(place[:], src[:, 0:wide].rearrange(
                        "p (m e) -> p m e", e=NE), free[:].unsqueeze(1).broadcast_to(
                            [P, TILES, NE]), ALU.add), s)
                    dve.tensor_tensor(free[:], free[:], src[:, wide:wide + NE], ALU.add)\
                        .then_inc(left["prefix"], 1)
                    link(dve.tensor_tensor(place[:], place[:], onehot[:], ALU.mult), s)
                    link(dve.tensor_reduce(placef[:], place[:], AX.X, ALU.add), s)
                    if not w.early():
                        dve.wait_ge(scattered[w.par], w.pair_count(16 * TILES) - 16 * TILES)
                    dve.tensor_copy(placeu[w.par][:], placef[:]).then_inc(v["place"], 1)
                    dve.wait_ge(left["prefix"], w.count(1, 1))

            def step(s, j):
                if s.first() and j == 0:
                    dve.wait_ge(xp_done, 1)
                else:
                    dve.wait_ge(stepped, s.count(SIDE, j))
                base = (j % (2 * GROUP)) // 2 * 2 * B
                sums = rbank[j % 2][:, base:base + 2 * B].rearrange(
                    "p (m b) -> p m b", b=B)
                parts = hparts[j % 2]
                dve.tensor_scalar(parts[:, 0, :, :], sums, 0.0, None, ALU.max)\
                    .then_inc(part_done[0], 1)
                dve.wait_ge(part_done[0], s.count(SIDE, j + 1))
                dve.scalar_tensor_tensor(parts[:, 1, :, :], sums, 0.0, parts[:, 0, :, :],
                                         ALU.max, ALU.subtract).then_inc(part_done[1], 1)
                dve.scalar_tensor_tensor(rest[:], sums, 0.0, parts[:, 0, :, :],
                                         ALU.max, ALU.subtract).then_inc(rest_done, 1)
                dve.wait_ge(part_done[1], s.count(SIDE, j + 1))
                dve.wait_ge(rest_done, s.count(SIDE, j + 1))
                dve.tensor_tensor(parts[:, 2, :, :], rest[:], parts[:, 1, :, :], ALU.subtract)\
                    .then_inc(part_done[2], 1)

            all_slots(dve, piece, step, lambda: links_before.append(links_before.pop() + links[0]),
                      steady)

            count, tiles, ends, starts, one = (row8[n][:] for n in (
                "count", "tiles", "ends", "starts", "one"))
            dve.tensor_copy(freeu[:], free[0:1, :]).then_inc(ends_known, 1)
            link(dve.tensor_tensor(count, free[0:1, :], region[0:1, :], ALU.subtract))
            link(dve.tensor_scalar(count, count, float(TS - 1), None, ALU.add))
            link(dve.tensor_copy(row8i[:], count))
            link(dve.tensor_single_scalar(row8i[:], row8i[:], TS.bit_length() - 1,
                                          ALU.logical_shift_right))
            link(dve.tensor_copy(tiles, row8i[:]))
            link(dve.tensor_tensor_scan(ends, one, tiles, 0.0, ALU.mult, ALU.add))
            link(dve.tensor_tensor(starts, ends, tiles, ALU.subtract))
            wide = [1, NTILES, NE]

            def over_tiles(a):
                return a.unsqueeze(1).broadcast_to(wide)

            a, b = tab["a"], tab["b"]
            link(dve.tensor_tensor(a[:], tilex[:], over_tiles(starts), ALU.is_ge))
            link(dve.tensor_tensor(b[:], tilex[:], over_tiles(ends), ALU.is_lt))
            link(dve.tensor_tensor(a[:], a[:], b[:], ALU.mult))
            link(dve.tensor_reduce(tilef["any"][:], a[:], AX.X, ALU.add))
            link(dve.tensor_tensor(b[:], tilex[:], over_tiles(starts), ALU.subtract))
            link(dve.scalar_tensor_tensor(b[:], b[:], float(TS), over_tiles(region[0:1, :]),
                                          ALU.mult, ALU.add))
            link(dve.tensor_tensor(b[:], b[:], a[:], ALU.mult))
            link(dve.tensor_reduce(tilef["place"][:], b[:], AX.X, ALU.add))
            link(dve.tensor_scalar(tilef["any"][:], tilef["any"][:], -1.0, 1.0,
                                   ALU.mult, ALU.add))
            link(dve.scalar_tensor_tensor(tilef["place"][:], tilef["any"][:],
                                          free[0:1, NE - 1:NE], tilef["place"][:],
                                          ALU.mult, ALU.add))
            dve.tensor_copy(tileu[:], tilef["place"][:]).then_inc(tables_done, 1)

            def tile_hidden(t, i, first):
                dve.wait_ge(t_h, 2 * t + 2)
                if not first:
                    dve.wait_ge(t_y, t - 1)
                dve.tensor_scalar(hid[i % 2][:, 1, :], pbank[1][:, 0:TS],
                                  wexp[i][:, 4 * P + 1:4 * P + 2], 0.0, ALU.add, ALU.max)\
                    .then_inc(t_hid1, 1)

            def tile_fin(t, i, first):
                n = i % NFIN
                if first:
                    dve.wait_ge(t_o, t + 1)
                else:
                    dve.wait_ge(out_done[n], first_use(t, n))
                    dve.wait_ge(t_o, t + 1)
                dve.tensor_copy(fid[n][:], rows[i][:, :, 2 * P]).then_inc(t_ids, 1)
                dve.wait_ge(t_ids, t + 1)
                dve.tensor_tensor(fin[n][:], rows[i][:, :, P:2 * P],
                                  rbank[i % 2][:, 0:TS].rearrange("p (m f) -> p m f", f=P),
                                  ALU.add).then_inc(t_fin, 1)

            def first_use(t, n):
                return (t - n) * (16 * MT // NFIN)

            for t in range(NBUF):
                tile_hidden(t, t, t < 2)
                if t:
                    tile_fin(t - 1, t - 1, t <= NFIN)
            with dve.Fori(NBUF, NTILES - NBUF + 1, NBUF) as t:
                for i in range(NBUF):
                    tile_hidden(t + i, i, False)
                    tile_fin(t + i - 1, (i - 1) % NBUF, False)
            tile_fin(NTILES - 1, NBUF - 1, False)


def patch_rows(x):
    t = np.asarray(x).reshape(B, 3, SIDE, PATCH, SIDE, PATCH).transpose(2, 1, 3, 5, 0, 4)
    return np.ascontiguousarray(t.reshape(SIDE, KC, P, ROW).transpose(0, 2, 1, 3))


def patch_weights(w_main, w_sx, w_sy):
    d, ds, h = w_main.shape[0], w_sx.shape[0], PATCH // 2
    w = np.zeros((d + 4 * ds, 3, PATCH, PATCH), w_main.dtype)
    w[:d] = w_main.reshape(d, 3, PATCH, PATCH)
    sx, sy = (a.reshape(ds, 3, PATCH, PATCH) for a in (w_sx, w_sy))
    w[d:d + ds, :, :, h:] = sx[:, :, :, :h]
    w[d + ds:d + 2 * ds, :, :, :h] = sx[:, :, :, h:]
    w[d + 2 * ds:d + 3 * ds, :, h:, :] = sy[:, :, :h, :]
    w[d + 3 * ds:, :, :h, :] = sy[:, :, h:, :]
    return np.ascontiguousarray(w.reshape(-1, KC, P).transpose(2, 1, 0))


def kernel(**inputs):
    import concourse.bacc as bacc
    from concourse.bass_utils import run_bass_kernel_spmd

    a = {k: np.asarray(t) for k, t in inputs.items()}
    f = a["x"].dtype
    tok, at, rn, ff = "L0_tok_", "L0_attn_", "L1_attn_", "L1_ffn_"
    columns = [np.concatenate([a[tok + "b_main"], a[tok + "b_sx"], a[tok + "b_sx"],
                               a[tok + "b_sy"], a[tok + "b_sy"]]),
               a[at + "A"], a[at + "bias_h"], a[at + "bias_y"],
               a[rn + "b_out"]]
    w1 = a[ff + "W1"]
    w2 = a[ff + "W2"].reshape(NE, 2, P, P).transpose(0, 2, 1, 3).reshape(NE, P, 2 * P)
    b1 = a[ff + "b1"].reshape(NE, 2, P).transpose(0, 2, 1)
    b2 = a[ff + "b2"][:, :, None]
    arrays = {
        "x": patch_rows(a["x"]),
        "w_tok": patch_weights(a[tok + "W_main"], a[tok + "W_sx"], a[tok + "W_sy"]),
        "w_attn": np.stack([a[at + n].T for n in ("Wg", "B", "C", "D")], 1),
        "vectors": np.stack(columns, 1),
        "rows_gb": np.broadcast_to(np.stack([a[tok + "ln_g"], a[tok + "ln_b"]]), (P, 2, P)),
        "w_ih": a[rn + "W_ih"].reshape(2, P, P).transpose(2, 0, 1),
        "w_hh": a[rn + "W_hh"].reshape(2, P, 2, P).transpose(3, 2, 0, 1),
        "w_out": a[rn + "W_out"].reshape(P, 2, P).transpose(2, 1, 0),
        "b_rnn": np.stack([a[rn + "b_ih"], a[rn + "b_hh"]])[None],
        "w_gate": a[ff + "Wg"],
        "b_gate": np.broadcast_to(a[ff + "bg"], (P, NE)),
        "ident": np.eye(P, dtype=f),
        "first_ids": np.arange(ROW, dtype=f).reshape(TILES, P).T,
        "triangle": np.triu(np.ones((P, P), f), 1),
        "experts": np.concatenate([w1, w2, b1, b2, np.zeros_like(b2)], 2),
    }
    arrays = {k: np.ascontiguousarray(t) for k, t in arrays.items()}
    nc = bacc.Bacc("TRN2", target_bir_lowering=False, num_devices=1)
    args = [nc.dram_tensor(f"in_{k}", t.shape, mybir.dt.from_np(t.dtype),
                           kind="ExternalInput").ap() for k, t in arrays.items()]
    places = nc.dram_tensor("places", (NE * CAP, WIDE), F32, kind="Internal").ap()
    out = nc.dram_tensor("out", (TOKENS, P), F32, kind="ExternalOutput").ap()
    build(nc, *args, places, out)
    r = run_bass_kernel_spmd(nc, [{f"in_{k}": t for k, t in arrays.items()}], core_ids=[0])
    got = np.asarray(r.results[0]["out"])
    got = got.reshape(SIDE, B, SIDE, P).transpose(1, 0, 2, 3)
    return np.ascontiguousarray(got.reshape(B, SIDE * SIDE, P))
```
